# Optimizing a Trainium2 kernel written in Bass

```python
import numpy as np
import jax
import jax.numpy as jnp

def _softmax(x, axis=-1):
    return jax.nn.softmax(x, axis=axis)

def _gelu(x):
    return jax.nn.gelu(x, approximate=True)

def _silu(x):
    return jax.nn.silu(x)

def _sigmoid(x):
    return jax.nn.sigmoid(x)

def _layernorm(x, axis=-1, eps=1e-05):
    m = jnp.mean(x, axis=axis, keepdims=True)
    v = jnp.var(x, axis=axis, keepdims=True)
    return (x - m) / jnp.sqrt(v + eps)

def _scatter_add(tgt, idx, src, axis=0):
    return tgt.at[idx].add(src)

def _segment_sum(src, seg, n):
    return jax.ops.segment_sum(src, seg, n)
kernel_name = 'mk_adj_resnorm_d4_adj_r2_b1cbf4'

def setup_inputs(seed: int=0):
    np.random.seed(seed)
    _w = jnp.asarray

    def _rec_inputs():
        import jax
        import jax.numpy as jnp
        _gk = jax.random.key(seed)
        x = -0.0002928 + 1 * jax.random.normal(jax.random.fold_in(_gk, 1), (8, 1024, 128), jnp.float32)
        _w = (1.0 + jnp.arange(1024, dtype=jnp.float32)) ** (-0.5)
        _w = _w / _w.mean()
        _pij = jnp.clip(0.015625 * _w[:, None] * _w[None, :], 0.0, 1.0)
        _a = jax.random.uniform(jax.random.fold_in(_gk, 2), (1024, 1024)) < _pij
        _af = _a.astype(jnp.float32)
        adj = _af
        return (x, adj)
    x, adj = _rec_inputs()

    def _L0_gnn_setup():
        import jax, jax.numpy as jnp
        import numpy as np
        B, N, C, D = (8, 1024, 128, 128)
        NEG = -1e+16
        key = jax.random.key(seed)
        k1, k2, k3, k4, k5 = jax.random.split(key, 5)
        inputs = jax.random.normal(k1, (B, N, C), dtype=jnp.float32)
        graph = jax.random.bernoulli(k2, 0.5, (N, N)).astype(jnp.float32)
        W = jax.random.normal(k3, (C, D), dtype=jnp.float32) * (1.0 / np.sqrt(C))
        b_lin = jax.random.normal(k4, (D,), dtype=jnp.float32) * 0.02
        b = jax.random.normal(k5, (D,), dtype=jnp.float32)
        return {'inputs': inputs, 'graph': graph, 'W': W, 'b_lin': b_lin, 'b': b}
    _L0_gnn_all = _L0_gnn_setup()
    _L0_gnn_in = {k: v for k, v in _L0_gnn_all.items() if k in ('W', 'b_lin', 'b')}
    del _L0_gnn_all

    def _L1_gnn_setup():
        import jax, jax.numpy as jnp
        import numpy as np
        EPS = 1e-05

        def _batchnorm(x, gamma, beta):
            mu = jnp.mean(x, axis=0)
            var = jnp.var(x, axis=0)
            return (x - mu) * jax.lax.rsqrt(var + EPS) * gamma + beta
        key = jax.random.key(seed)
        ks = jax.random.split(key, 4)
        b, n, d, h, o = (32, 1024, 128, 256, 128)
        features = jax.random.normal(ks[0], (b, n, d), dtype=jnp.float32)
        A = jax.random.uniform(ks[1], (n, n), dtype=jnp.float32)
        lim1 = float(np.sqrt(6.0 / (d + h)))
        W1 = jax.random.uniform(ks[2], (h, d), minval=-lim1, maxval=lim1, dtype=jnp.float32)
        b1 = jnp.zeros((h,), jnp.float32)
        lim2 = float(np.sqrt(6.0 / (h + o)))
        W2 = jax.random.uniform(ks[3], (o, h), minval=-lim2, maxval=lim2, dtype=jnp.float32)
        b2 = jnp.zeros((o,), jnp.float32)
        g1 = jnp.ones((h,), jnp.float32)
        be1 = jnp.zeros((h,), jnp.float32)
        g2 = jnp.ones((o,), jnp.float32)
        be2 = jnp.zeros((o,), jnp.float32)
        return {'features': features, 'A': A, 'W1': W1, 'b1': b1, 'g1': g1, 'be1': be1, 'W2': W2, 'b2': b2, 'g2': g2, 'be2': be2}
    _L1_gnn_all = _L1_gnn_setup()
    _L1_gnn_in = {k: v for k, v in _L1_gnn_all.items() if k in ('W1', 'b1', 'g1', 'be1', 'W2', 'b2', 'g2', 'be2')}
    del _L1_gnn_all

    def _L2_gnn_setup():
        import jax, jax.numpy as jnp
        import numpy as np
        B, J, F_IN, F_OUT = (8192, 17, 128, 128)
        key = jax.random.key(seed)
        k1, k2, k3, k4 = jax.random.split(key, 4)
        gain = 1.414
        bound = gain * np.sqrt(6.0 / (F_IN + F_OUT))
        W = jax.random.uniform(k2, (3, F_IN, F_OUT), dtype=jnp.float32, minval=-bound, maxval=bound)
        stdv = 1.0 / np.sqrt(F_OUT)
        bias = jax.random.uniform(k4, (F_OUT,), dtype=jnp.float32, minval=-stdv, maxval=stdv)
        return {'x': jax.random.normal(k1, (B, J, F_IN), dtype=jnp.float32), 'W': W, 'adj': jax.random.uniform(k3, (J, J), dtype=jnp.float32), 'bias': bias}
    _L2_gnn_all = _L2_gnn_setup()
    _L2_gnn_in = {k: v for k, v in _L2_gnn_all.items() if k in ('W', 'bias')}
    del _L2_gnn_all

    def _L3_gnn_setup():
        import jax, jax.numpy as jnp
        import numpy as np
        ALPHA = 0.2
        key = jax.random.key(seed)
        k1, k2, k3, k4 = jax.random.split(key, 4)
        B, N, Fin, Fout = (8, 1024, 128, 128)
        h = jax.random.normal(k1, (B, N, Fin), dtype=jnp.float32)
        adj = jax.random.randint(k2, (N, N), 0, 2).astype(jnp.float32)
        adj = jnp.maximum(adj, jnp.eye(N, dtype=jnp.float32))

        def xavier(k, shape, gain=1.414):
            fan_in, fan_out = (shape[0], shape[1])
            a = gain * np.sqrt(6.0 / (fan_in + fan_out))
            return jax.random.uniform(k, shape, dtype=jnp.float32, minval=-a, maxval=a)
        W = xavier(k3, (Fin, Fout))
        a = xavier(k4, (2 * Fout, 1))
        return {'h': h, 'adj_matrix': adj, 'W': W, 'a': a}
    _L3_gnn_all = _L3_gnn_setup()
    _L3_gnn_in = {k: v for k, v in _L3_gnn_all.items() if k in ('W', 'a')}
    del _L3_gnn_all
    return {'x': x, 'adj': adj, 'L0_gnn_W': _L0_gnn_in['W'], 'L0_gnn_b_lin': _L0_gnn_in['b_lin'], 'L0_gnn_b': _L0_gnn_in['b'], 'L1_gnn_W1': _L1_gnn_in['W1'], 'L1_gnn_b1': _L1_gnn_in['b1'], 'L1_gnn_g1': _L1_gnn_in['g1'], 'L1_gnn_be1': _L1_gnn_in['be1'], 'L1_gnn_W2': _L1_gnn_in['W2'], 'L1_gnn_b2': _L1_gnn_in['b2'], 'L1_gnn_g2': _L1_gnn_in['g2'], 'L1_gnn_be2': _L1_gnn_in['be2'], 'L2_gnn_W': _L2_gnn_in['W'], 'L2_gnn_bias': _L2_gnn_in['bias'], 'L3_gnn_W': _L3_gnn_in['W'], 'L3_gnn_a': _L3_gnn_in['a']}

def reference(x, adj, L0_gnn_W, L0_gnn_b_lin, L0_gnn_b, L1_gnn_W1, L1_gnn_b1, L1_gnn_g1, L1_gnn_be1, L1_gnn_W2, L1_gnn_b2, L1_gnn_g2, L1_gnn_be2, L2_gnn_W, L2_gnn_bias, L3_gnn_W, L3_gnn_a):
    import jax
    import jax.numpy as jnp

    def _L0_gnn_ref(inputs, graph, W, b_lin, b):
        import jax, jax.numpy as jnp
        import numpy as np
        B, N, C, D = (8, 1024, 128, 128)
        NEG = -1e+16
        h = jnp.einsum('bnc,cd->bnd', inputs, W) + b_lin
        scores = jnp.einsum('bnd,bmd->bnm', h, h) * graph[None, :, :]
        scores = jnp.where(scores == 0.0, NEG, scores)
        attention = jax.nn.softmax(scores, axis=2)
        return jnp.einsum('bnm,bmd->bnd', attention, h) + b

    def _L1_gnn_ref(features, A, W1, b1, g1, be1, W2, b2, g2, be2):
        import jax, jax.numpy as jnp
        import numpy as np
        EPS = 1e-05

        def _batchnorm(x, gamma, beta):
            mu = jnp.mean(x, axis=0)
            var = jnp.var(x, axis=0)
            return (x - mu) * jax.lax.rsqrt(var + EPS) * gamma + beta
        b, n, d = features.shape
        A_norm = A + jnp.eye(n, dtype=A.dtype)
        deg = jnp.sum(A_norm, axis=0) + jnp.sum(A_norm, axis=1) - jnp.diagonal(A_norm)
        dinv = jax.lax.rsqrt(deg)
        A_hat = A_norm * dinv[:, None] * dinv[None, :]
        agg = jnp.einsum('nm,bmd->bnd', A_hat, features)
        x = agg.reshape(-1, d)
        h = jax.nn.relu(_batchnorm(x @ W1.T + b1, g1, be1))
        out = h @ W2.T + b2
        out = _batchnorm(out, g2, be2)
        return out.reshape(b, n, -1)

    def _L2_gnn_ref(x, W, adj, bias):
        import jax, jax.numpy as jnp
        import numpy as np
        B, J, F_IN, F_OUT = (8192, 17, 128, 128)
        adj_0 = jnp.diag(jnp.diagonal(adj))
        adj_1 = jnp.triu(adj, k=1)
        adj_2 = jnp.tril(adj, k=-1)
        h = jnp.einsum('bjf,kfo->kbjo', x, W)
        out = jnp.einsum('ij,bjo->bio', adj_0, h[0]) + jnp.einsum('ij,bjo->bio', adj_1, h[1]) + jnp.einsum('ij,bjo->bio', adj_2, h[2])
        return out + bias[None, None, :]

    def _L3_gnn_ref(h, adj_matrix, W, a):
        import jax, jax.numpy as jnp
        import numpy as np
        ALPHA = 0.2
        Fout = W.shape[1]
        Wh = jnp.einsum('bnf,fo->bno', h, W)
        a1, a2 = (a[:Fout, 0], a[Fout:, 0])
        s1 = Wh @ a1
        s2 = Wh @ a2
        e = s1[:, :, None] + s2[:, None, :]
        e = jnp.where(e >= 0, e, ALPHA * e)
        e = jnp.where(adj_matrix[None] == 0, -jnp.inf, e)
        attention = jax.nn.softmax(e, axis=-1)
        h_prime = jnp.einsum('bij,bjo->bio', attention, Wh)
        return h_prime
    x = _layernorm(x + _L0_gnn_ref(x, adj, L0_gnn_W, L0_gnn_b_lin, L0_gnn_b), axis=-1)
    x = _layernorm(x + _L1_gnn_ref(x, adj, L1_gnn_W1, L1_gnn_b1, L1_gnn_g1, L1_gnn_be1, L1_gnn_W2, L1_gnn_b2, L1_gnn_g2, L1_gnn_be2), axis=-1)
    x = _layernorm(x + _L2_gnn_ref(x, L2_gnn_W, adj, L2_gnn_bias), axis=-1)
    x = _layernorm(x + _L3_gnn_ref(x, adj, L3_gnn_W, L3_gnn_a), axis=-1)
    return x

_drawn_inputs = setup_inputs


def setup_inputs(seed=0):
    import zlib

    import numpy as np

    out = dict(_drawn_inputs(seed))
    spreads = {'L1_gnn_b1': (0.0, 0.8),
     'L1_gnn_g1': (1.0, 0.2),
     'L1_gnn_be1': (0.0, 0.1),
     'L1_gnn_b2': (0.0, 0.8),
     'L1_gnn_g2': (1.0, 0.2),
     'L1_gnn_be2': (0.0, 0.1)}
    factors = {'L2_gnn_bias': 8.0}
    for name, (base, spread) in spreads.items():
        noise = np.random.default_rng([zlib.crc32(name.encode()), seed]).standard_normal(out[name].shape)
        drawn = base * np.exp(spread * noise) if base else spread * noise
        out[name] = jnp.asarray(drawn.astype(out[name].dtype))
    for name, factor in factors.items():
        out[name] = (out[name] * factor).astype(out[name].dtype)
    return out
```

```python
from contextlib import ExitStack

import concourse.bass as bass
from concourse import mybir

P = 128
EPS = 1e-5
NEG = 1e16
BIG = 1e30
NCONST = 11
CLAMP = 1e20
F32, F32R, BF16 = mybir.dt.float32, mybir.dt.float32r, mybir.dt.bfloat16
ALU, ACT = mybir.AluOpType, mybir.ActivationFunctionType
EQ = ALU.is_equal


class Batch:

    def __init__(self, b, n, p, count):
        self.b, self.n, self.p = b, n, p
        known = isinstance(b, int)
        self.prev = not known or b >= 1
        self.cur = not known or 0 <= b < count
        self.nxt = not known or b < count - 1
        self.index = b if known else None


def for_batches(eng, count, body):
    body(Batch(-1, -1, 1, count))
    body(Batch(0, 0, 0, count))
    with eng.Fori(0, (count - 2) // 2) as i:
        body(Batch(i * 2 + 1, i, 1, count))
        body(Batch(i * 2 + 2, i + 1, 0, count))
    body(Batch(count - 1, (count - 1) // 2, 1, count))
    body(Batch(count, count // 2, 0, count))


def graph_layers(nc, a, out):
    B, N, C = a["x"].shape
    NT = N // P
    HT = NT // 2
    HN = N // 2
    HB = a["w1t"].shape[1] // P
    assert C == P and NT == 8 and HB == 2 and B % 2 == 0

    with ExitStack() as ctx:
        def sb(name, shape, dt=F32):
            return ctx.enter_context(nc.sbuf_tensor(name, shape, dt))

        def sem(name):
            return ctx.enter_context(nc.semaphore(name))

        X = sb("X", [P, B, NT, C])
        AT = sb("AT", [P, NT, N], F32R)
        DU = sb("DU", [P, NT, P], F32R)
        DL = sb("DL", [P, NT, P], F32R)
        DD = sb("DD", [P, NT, P], F32R)
        G = sb("G", [P, NT, N], BF16)
        FR = sb("FR", [P, 2, 2, N], F32R)
        arena = sb("arena", [P, 84 * 256])
        dinvb = sb("dinvb", [P, N])
        ident = sb("ident", [P, P])
        w0, w3 = sb("w0", [P, C]), sb("w3", [P, C])
        w1t, w2t, wl2 = sb("w1tS", [P, HB * P]), sb("w2tS", [P, HB, C]), sb("wl2S", [P, 3, C])
        w3t = sb("w3tS", [P, C])
        bias0, bias0b, bias2 = sb("bias0", [P, C]), sb("bias0b", [P, C]), sb("bias2", [P, C])
        cols = sb("cols", [P, 12])
        acol = sb("acol", [P, 2])
        wa = sb("wa", [P, 4])
        epsc = sb("epsc", [P, 1])
        negmax = sb("negmax", [P, 2 * NT])
        sums = sb("sums", [P, 2 * NT])
        rsum = sb("rsum", [P, NT])
        small = sb("small", [P, 2, NT])
        stats = sb("stats", [P, 2, NT, 6])
        mv = sb("mv", [P, 2, NT, 2])
        newt = sb("newt", [P, 2, 4, NT])
        rstd = sb("rstd", [P, 2, NT])
        nbias = sb("nbias", [P, 2, NT])
        deg = sb("deg", [P, 4, NT])
        dinv = sb("dinv", [P, NT])
        bnst = sb("bnst", [P, HB, 2 * B, 6])
        bnmv = sb("bnmv", [P, HB, 2])
        bnsc = sb("bnsc", [P, 6, HB])
        scol = sb("scol", [P, 2, NT, 4])

        def region(kb, size_kb):
            return arena[:, kb * 256:(kb + size_kb) * 256]

        bnst2 = bnst[:].rearrange("p h a b -> p (h a b)")
        xin = a["x"].rearrange("b (t p) c -> p (b t) c", p=P)
        outv = out.rearrange("b (t p) c -> p (b t) c", p=P)
        X2 = X[:].rearrange("p b t c -> p (b t c)")
        xs = region(0, 8).rearrange("p (q t c) -> p q t c", q=2, c=C)
        xT = region(8, 4)
        hN = region(12, 8).rearrange("p (q t c) -> p q t c", q=2, c=C)
        T = region(20, 16).rearrange("p (q n) -> p q n", q=4)
        U = region(36, 8).rearrange("p (q n) -> p q n", q=2)
        PT = region(44, 32).rearrange("p (q m n) -> p q m n", q=2, m=NT)
        OT = region(76, 4).rearrange("p (q n) -> p q n", q=2)
        Y = region(80, 4).rearrange("p (q t c) -> p q t c", q=2, c=C)
        Z1 = region(0, 64).rearrange("p (h n) -> p h n", h=HB)
        Z1f = region(0, 64)
        xsc = region(64, 8).rearrange("p (q t c) -> p q t c", q=2, c=C)
        agS = region(72, 8).rearrange("p (q n) -> p q n", q=2)
        UDL = region(32, 24).rearrange("p (q k n) -> p q k n", q=2, k=3)
        zn = region(56, 4)
        Yc = region(60, 4).rearrange("p (t c) -> p t c", c=C)
        xb2 = region(64, 8).rearrange("p (q t c) -> p q t c", q=2, c=C)

        blin, b1c, g1c, be1c, b2c, g2c, be2c = (
            cols[:, 0:1], cols[:, 1:3], cols[:, 3:5], cols[:, 5:7], cols[:, 7:8], cols[:, 8:9], cols[:, 9:10])

        def ps(name, shape):
            return ctx.enter_context(nc.psum_tensor(name, shape, F32))

        psS = [ps("psS0", [P, N]), ps("psS1", [P, N])]
        psT = [ps("psT0", [P, HN]), ps("psT1", [P, HN])]
        psO, psB = ps("psO", [P, HN]), ps("psB", [P, HN])

        consts_in, ident_ok, setup_ok, g_cast, at_cast, tri_ok, bias0_ok, wa_ps, wa_ok, g3_ok = (
            sem(n) for n in ("consts_in", "ident_ok", "setup_ok", "g_cast", "at_cast", "tri_ok", "bias0_ok",
                             "wa_ps", "wa_ok", "g3_ok"))
        g_in = [sem(f"g_in{i}") for i in range(4)]
        at_in = [sem(f"at_in{i}") for i in range(4)]
        gate = sem("gate")
        diag_ok, dg_ok, dg_l, dg_ln, dg_step, dinv_ok, db_ps, dinvb_ok = (
            sem(n) for n in ("diag_ok", "dg_ok", "dg_l", "dg_ln", "dg_step", "dinv_ok", "db_ps", "dinvb_ok"))
        (xsc_ok, ahi_ok, alo_ok, ag_ps, ag_ok, z_ps, z_ok, zst_ok, bn1_mv, bn1_l, bn1_ln, bn1_step, bn1_nw, bn1_ok,
         relu_ok, z2_ps, z2_ok, z2st_ok, bn2_mv, bn2_l, bn2_ln, bn2_step, bn2_nw, bn2_ok) = (
            sem(n) for n in ("xsc_ok ahi_ok alo_ok ag_ps ag_ok z_ps z_ok zst_ok bn1_mv bn1_l bn1_ln bn1_step bn1_nw "
                             "bn1_ok relu_ok z2_ps z2_ok z2st_ok bn2_mv bn2_l bn2_ln bn2_step bn2_nw bn2_ok").split())
        (zn_ok, c_ps, c_y, c_bn, c_mv, c_l, c_ln, c_step, c_nw, c_x, e_hi, e_lo, e_xb, e_ps, e_ok, e_out, e_y,
         e_bn, e_mv, e_l, e_ln, e_step, e_nw, e_x) = (
            sem(n) for n in ("zn_ok c_ps c_y c_bn c_mv c_l c_ln c_step c_nw c_x e_hi e_lo e_xb e_ps e_ok e_out e_y "
                             "e_bn e_mv e_l e_ln e_step e_nw e_x").split())

        def att_semaphores(tag):
            names = ("scores_done mask_done zero_done w_done exp_done tr_done pt_done pv_done ot_done back_done "
                     "bn_done lnexp_done newt_done norm_done xt_ps xt_ok ht_ps hi_ok lo_ok hn_ps hn_ok xb_ok u_ok "
                     "s_ps s_ok sb_ps nm_ok rs_ok mv_ok l_ok newt_step y0_ok").split()
            sems = {n: sem(f"{tag}_{n}") for n in names}
            sems["x_in"] = [sem(f"{tag}_x_in{i}") for i in range(2)]
            sems["out_ok"] = [sem(f"{tag}_out_ok{i}") for i in range(2)]
            return sems

        A0, A3 = att_semaphores("l0"), att_semaphores("l3")

        block = ctx.enter_context(nc.Block())

        def v4(t):
            return t.rearrange("p (t c) -> p t c", c=C)

        def xrow(b, t):
            return X2[:, bass.ds(b * N + t * C, C)]

        def zrow(h, b, c0, n):
            return Z1f[:, bass.ds(b * N + (h * B * N + c0), n)]

        def xall(b):
            return X2[:, bass.ds(b * N, N)]

        def alone(eng):
            eng.sem_inc(gate, 1)


        Y_AT = {0: (2, 6), 3: (4, 7)}
        LN_EXP_AT = {0: (3, 6), 3: (3, 7)}
        REFINE_AT = {0: (5, 7), 3: (6, 7)}
        NORM_AT = {0: (5, 7), 3: (5, 7)}

        def att_pe(pe, L, A):
            w_val = w0 if L == 0 else w3

            def scores(q, r, s):
                hi, lo = FR[:, q, 0], FR[:, q, 1]
                cs = slice(r * P, (r + 1) * P)
                for ch in range(2):
                    o = psS[r % 2][:, ch * HN:(ch + 1) * HN]
                    cc = slice(ch * HN, (ch + 1) * HN)
                    nc.tensor.matmul(o, hi[:, cs], hi[:, cc], start=True, stop=False)
                    nc.tensor.matmul(o, hi[:, cs], lo[:, cc], start=False, stop=False)
                    mm = nc.tensor.matmul(o, lo[:, cs], hi[:, cc], start=False, stop=True)
                mm.then_inc(A["scores_done"], 1)

            def body(k):
                b, p = k.b, k.p
                for r in range(NT):
                    s = b * NT + r
                    if L == 0 and (k.cur if r < NT - 1 else k.nxt):
                        if r == NT - 1:
                            pe.wait_ge(A["lo_ok"], b * 2 + 4)
                        if k.prev or (k.cur and r >= 1):
                            pe.wait_ge(A["mask_done"], s)
                        if r < NT - 1:
                            scores(p, r + 1, s + 1)
                        else:
                            scores(1 - p, 0, s + 1)
                    if k.prev and r == 0 or k.cur and r >= 1:
                        tile = (r - 1) % NT
                        pe.wait_ge(A["exp_done"], s)
                        for half in range(2):
                            if k.prev or r >= 2:
                                pe.wait_ge(A["pt_done"], s * 2 - 3 + half)
                            for m in range(HT):
                                blk = half * HT + m
                                tr = nc.tensor.transpose(psT[half][:, m * P:(m + 1) * P],
                                                         T[:, tile % 4, blk * P:(blk + 1) * P], ident[:])
                            tr.then_inc(A["tr_done"], 1)
                    if (k.prev and r <= 4) or (k.cur and r >= 5):
                        j = (r - 1) % 4
                        if j == 0:
                            half_no = b * 2 + (r - 1) // 4 - 1
                            pe.wait_ge(A["pt_done"], b * 16 + (r - 1) * 2)
                            if k.prev:
                                pe.wait_ge(A["ot_done"], half_no)
                            if r == 5:
                                pe.wait_ge(A["hn_ok"], b * 2 + 2)
                        q = p if r >= 5 else 1 - p
                        hq = (((r - 1) // 4) - 1) % 2
                        for m in (2 * j, 2 * j + 1):
                            mm = nc.tensor.matmul(psO[:], hN[:, q, m, :], PT[:, hq, m, :],
                                                  start=(m == 0), stop=(m == NT - 1))
                        if j == 3:
                            mm.then_inc(A["pv_done"], 1)
                    if r in (1, 5) and k.prev:
                        half_no = b * 2 - 2 + r // 4
                        pe.wait_ge(A["ot_done"], half_no + 1)
                        if r == 1 and k.nxt:
                            pe.wait_ge(A["xt_ok"], b * 2 + 3)
                        elif r == 1 and k.index == B - 1:
                            pe.wait_ge(A["hn_ok"], B * 2)
                        elif k.nxt:
                            pe.wait_ge(A["lo_ok"] if L == 0 else A["s_ok"], b * 2 + 4 if L == 0 else b + 2)
                        else:
                            pe.wait_ge(A["y0_ok"], half_no)
                        for t in range(HT):
                            tr = nc.tensor.transpose(psB[:, t * P:(t + 1) * P],
                                                     OT[:, r // 4, t * P:(t + 1) * P], ident[:])
                        tr.then_inc(A["back_done"], 1)
                    if not k.nxt:
                        continue
                    if r in (0, 2):
                        if r == 0:
                            pe.wait_ge(A["x_in"][1 - p], (k.n + (1 if p else 0)) * 16 + 16)
                            if k.cur:
                                pe.wait_ge(A["hn_ok"], b * 2 + 2)
                        elif k.prev:
                            pe.wait_ge(A["y0_ok"], b * 2 - 1)
                        elif r == 2:
                            pe.wait_ge(A["xt_ok"], b * 2 + 3)
                        for t in range(HT):
                            tr = nc.tensor.transpose(psB[:, t * P:(t + 1) * P],
                                                     xs[:, 1 - p, r // 2 * HT + t, :], ident[:])
                        tr.then_inc(A["xt_ps"], 1)
                    if L == 0 and r in (3, 4):
                        if r == 3:
                            pe.wait_ge(A["xt_ok"], b * 2 + 4)
                        else:
                            pe.wait_ge(A["lo_ok"], b * 2 + 3)
                        nc.tensor.matmul(psB[:], w0[:], xT[:, (r - 3) * HN:(r - 2) * HN],
                                         start=True, stop=True).then_inc(A["ht_ps"], 1)
                    if L == 3 and r == 3:
                        pe.wait_ge(A["xt_ok"], b * 2 + 4)
                        for t in range(NT):
                            mm = nc.tensor.matmul(psB[:, t * 4:t * 4 + 4], xT[:, t * P:(t + 1) * P], wa[:],
                                                  start=True, stop=True)
                        mm.then_inc(A["s_ps"], 1)
                    if L == 3 and r == 4:
                        pe.wait_ge(A["s_ok"], b + 2)
                        if k.prev:
                            pe.wait_ge(A["mask_done"], b * NT)
                        for t in range(NT):
                            tr = nc.tensor.transpose(psS[1 - p][:, t * P:(t + 1) * P],
                                                     scol[:, 1 - p, t, 2:3].broadcast_to([P, P]), ident[:])
                        tr.then_inc(A["sb_ps"], 1)
                    if r in (6, 7):
                        if r == 7:
                            pe.wait_ge(A["hn_ok"], b * 2 + 3)
                        elif k.prev:
                            pe.wait_ge(A["y0_ok"], b * 2)
                        else:
                            pe.wait_ge(A["lo_ok"] if L == 0 else A["s_ok"], b * 2 + 4 if L == 0 else b + 2)
                        for t in range(HT):
                            tt = (r - 6) * HT + t
                            mm = nc.tensor.matmul(psB[:, t * P:(t + 1) * P], xT[:, tt * P:(tt + 1) * P],
                                                  w_val[:], start=True, stop=True)
                        mm.then_inc(A["hn_ps"], 1)

            for_batches(pe, B, body)

        def att_act(act, L, A):
            def aux(b, p, r, cur):
                if r in (0, 2):
                    act.wait_ge(A["xt_ps"], b * 2 + 3 + r // 2)
                    if r == 0 and cur:
                        act.wait_ge(A["hn_ps"], b * 2 + 2)
                    nc.scalar.copy(xT[:, r // 2 * HN:(r // 2 + 1) * HN], psB[:]).then_inc(A["xt_ok"], 1)
                if L == 0 and r in (3, 4):
                    act.wait_ge(A["ht_ps"], b * 2 + r)
                    nc.scalar.activation(FR[:, 1 - p, 0, (r - 3) * HN:(r - 2) * HN], psB[:], ACT.Identity,
                                         bias=blin).then_inc(A["hi_ok"], 1)
                if L == 3 and r == 3:
                    act.wait_ge(A["s_ps"], b + 2)
                    nc.scalar.copy(scol[:, 1 - p, :, :].rearrange("p t k -> p (t k)"),
                                   psB[:, 0:NT * 4]).then_inc(A["s_ok"], 1)
                if r in (6, 7):
                    act.wait_ge(A["hn_ps"], b * 2 + r - 3)
                    nc.scalar.copy(hN[:, 1 - p, (r - 6) * HT:(r - 5) * HT, :], v4(psB[:])).then_inc(A["hn_ok"], 1)

            def ln_exp(b, r):
                h = LN_EXP_AT[L].index(r)
                half_no = b * 2 - 2 + h
                act.wait_ge(A["mv_ok"], half_no + 1)
                nc.scalar.activation(newt[:, h, 0, 0:HT], mv[:, h, 0:HT, 1], ACT.Ln,
                                     bias=epsc[:]).then_inc(A["l_ok"], 1)
                act.wait_ge(A["l_ok"], half_no + 1)
                nc.scalar.activation(newt[:, h, 1, 0:HT], newt[:, h, 0, 0:HT], ACT.Exp,
                                     scale=-0.5).then_inc(A["lnexp_done"], 1)

            def exponentials(b, p, r):
                act.wait_ge(A["w_done"], b * NT + r + 1)
                i = p * NT + r
                nc.scalar.activation(T[:, r % 4, :], T[:, r % 4, :], ACT.Exp, bias=negmax[:, i:i + 1],
                                     scale=-1.0, accum_out=sums[:, i:i + 1]).then_inc(A["exp_done"], 1)

            def body(k):
                b, p = k.b, k.p
                for r in range(NT):
                    s = b * NT + r
                    if r >= 1 and k.nxt:
                        aux(b, p, r - 1, k.cur)
                    if r == 0 and k.cur:
                        aux(b - 1, 1 - p, NT - 1, k.prev)
                    if k.prev and r == 0 or k.cur and r >= 1:
                        j = (r - 1) % 4
                        hq = ((r - 1) // 4) % 2
                        if j == 0 and k.prev:
                            act.wait_ge(A["pv_done"], b * 2 + (r - 1) // 4 - 1)
                        for half in range(2):
                            act.wait_ge(A["tr_done"], s * 2 - 1 + half)
                            nc.scalar.copy(PT[:, hq, half * HT:(half + 1) * HT, j * P:(j + 1) * P],
                                           v4(psT[half][:])).then_inc(A["pt_done"], 1)
                    if L == 3 and k.prev and r in LN_EXP_AT[L]:
                        ln_exp(b, r)
                    if k.cur:
                        exponentials(b, p, r)
                    if L == 0 and k.prev and r in LN_EXP_AT[L]:
                        ln_exp(b, r)
                    if k.prev and r in (0, 4):
                        half_no = b * 2 - 2 + r // 4
                        act.wait_ge(A["pv_done"], half_no + 1)
                        nc.scalar.copy(OT[:, r // 4, :], psO[:]).then_inc(A["ot_done"], 1)
                    if k.prev and r in NORM_AT[L]:
                        h = NORM_AT[L].index(r)
                        half_no = b * 2 - 2 + h
                        act.wait_ge(A["newt_done"], half_no + 1)
                        alone(act)
                        for t in range(HT):
                            o = xrow(b - 1, h * HT + t) if L == 0 else Y[:, h, t, :]
                            n = nc.scalar.activation(o, Y[:, h, t, :], ACT.Identity, bias=nbias[:, h, t:t + 1],
                                                     scale=rstd[:, h, t:t + 1])
                        n.then_inc(A["norm_done"], 1)
                        if L == 3:
                            act.wait_ge(A["norm_done"], half_no + 1)
                            act.dma_start(outv[:, bass.ds((b - 1) * NT + h * HT, HT), :], Y[:, h]).then_inc(
                                A["out_ok"][h], 16)
                    if L == 0 and k.index == 0:
                        act.wait_ge(at_in[r // 2], 16)
                        nc.scalar.activation(AT[:, r, :], X[:, r].rearrange("p t c -> p (t c)"), ACT.Copy,
                                             accum_out=deg[:, 1, r:r + 1]).then_inc(at_cast, 1)
            for_batches(act, B, body)

        def att_dve(dve, L, A):
            def body(k):
                b, p = k.b, k.p
                for r in range(NT):
                    s = b * NT + r
                    i = p * NT + r
                    t_now = T[:, r % 4, :]
                    if k.cur and (k.prev or r >= 4):
                        dve.wait_ge(A["tr_done"], s * 2 - 6)
                    if L == 0 and k.cur:
                        if k.index == 0:
                            dve.wait_ge(g_cast, r + 1)
                        dve.wait_ge(A["scores_done"], s + 1)
                        nc.vector.tensor_tensor(t_now, psS[r % 2][:], G[:, r, :], ALU.mult).then_inc(A["mask_done"], 1)
                        dve.wait_ge(A["mask_done"], s + 1)
                        nc.vector.tensor_scalar(U[:, r % 2, :], t_now, 0.0, NEG, EQ, ALU.mult).then_inc(A["zero_done"], 1)
                        dve.wait_ge(A["zero_done"], s + 1)
                        alone(dve)
                        nc.vector.tensor_tensor_reduce(t_now, t_now, U[:, r % 2, :], 1.0, 3e38, ALU.add, ALU.min,
                                                       negmax[:, i:i + 1]).then_inc(A["w_done"], 1)
                    if L == 3 and k.cur:
                        if r == 0:
                            dve.wait_ge(A["sb_ps"], b + 1)
                        alone(dve)
                        nc.vector.tensor_tensor_reduce(t_now, psS[p][:], G[:, r, :], 1.0, 3e38, ALU.add, ALU.min,
                                                       small[:, 0, r:r + 1]).then_inc(A["mask_done"], 1)
                    if L == 3 and (k.cur and r >= 1 or k.prev and r == 0):
                        q, rl = (p, r - 1) if r else (1 - p, NT - 1)
                        dve.wait_ge(A["u_ok"], s)
                        nc.vector.scalar_tensor_tensor(T[:, rl % 4, :], T[:, rl % 4, :], scol[:, q, rl, 0:1],
                                                       U[:, rl % 2, :], ALU.add, ALU.min).then_inc(A["w_done"], 1)
                    if L == 3 and k.cur:
                        dve.wait_ge(A["mask_done"], s + 1)
                        nc.vector.tensor_scalar(small[:, 1, r:r + 1], small[:, 0, r:r + 1], scol[:, p, r, 0:1], CLAMP,
                                                ALU.add, ALU.min).then_inc(A["zero_done"], 1)
                        dve.wait_ge(A["zero_done"], s + 1)
                        nc.vector.scalar_tensor_tensor(negmax[:, i:i + 1], small[:, 1, r:r + 1], 0.2,
                                                       small[:, 1, r:r + 1], ALU.mult, ALU.min).then_inc(A["nm_ok"], 1)
                    if L == 0 and k.nxt and r in (4, 5):
                        cs = slice((r - 4) * HN, (r - 3) * HN)
                        dve.wait_ge(A["hi_ok"], b * 2 + r - 1)
                        nc.vector.scalar_tensor_tensor(FR[:, 1 - p, 1, cs], psB[:], blin,
                                                       FR[:, 1 - p, 0, cs].bitcast(F32), ALU.add,
                                                       ALU.subtract).then_inc(A["lo_ok"], 1)
                    if k.prev and r == 1:
                        dve.wait_ge(A["exp_done"], b * NT)
                        nc.vector.reciprocal(rsum[:], sums[:, (1 - p) * NT:(2 - p) * NT]).then_inc(A["rs_ok"], 1)
                    if k.prev and r in Y_AT[L]:
                        h = Y_AT[L].index(r)
                        half_no = b * 2 - 2 + h
                        dve.wait_ge(A["back_done"], half_no + 1)
                        if h == 0:
                            dve.wait_ge(A["rs_ok"], b)
                            if L == 0:
                                dve.wait_ge(A["xb_ok"], b)
                        if L == 3:
                            dve.wait_ge(A["out_ok"][h], b * 16)
                        alone(dve)
                        for t in range(HT):
                            y = nc.vector.scalar_tensor_tensor(Y[:, h, t, :], psB[:, t * P:(t + 1) * P],
                                                               rsum[:, h * HT + t:h * HT + t + 1],
                                                               xrow(b - 1, h * HT + t), ALU.mult, ALU.add)
                        y.then_inc(A["y0_ok"], 1)
                        dve.wait_ge(A["y0_ok"], half_no + 1)
                        for t in range(HT):
                            nc.vector.bn_stats(stats[:, h, t, :], Y[:, h, t, :]).then_inc(A["bn_done"], 1)
                        dve.wait_ge(A["bn_done"], half_no * HT + HT)
                        alone(dve)
                        for t in range(HT):
                            m = nc.vector.bn_aggr(mv[:, h, t, :], stats[:, h, t, :])
                        m.then_inc(A["mv_ok"], 1)
                    if k.prev and r in REFINE_AT[L]:
                        h = REFINE_AT[L].index(r)
                        half_no = b * 2 - 2 + h
                        dve.wait_ge(A["lnexp_done"], half_no + 1)
                        refine(dve, mv[:, h, 0:HT, 1], mv[:, h, 0:HT, 0], newt[:, h, :, 0:HT], rstd[:, h, 0:HT],
                               nbias[:, h, 0:HT], A["newt_step"], half_no, A["newt_done"])

            for_batches(dve, B, body)

        def refine(dve, var, mean, tmp, y_out, nb_out, step, turn, done, eps=EPS):
            y0, q, f = tmp[:, 1], tmp[:, 2], tmp[:, 3]
            nc.vector.tensor_tensor(q, y0, y0, ALU.mult).then_inc(step, 1)
            dve.wait_ge(step, turn * 4 + 1)
            nc.vector.scalar_tensor_tensor(f, var, eps, q, ALU.add, ALU.mult).then_inc(step, 1)
            dve.wait_ge(step, turn * 4 + 2)
            nc.vector.tensor_scalar(q, f, -0.5, 1.5, ALU.mult, ALU.add).then_inc(step, 1)
            dve.wait_ge(step, turn * 4 + 3)
            nc.vector.tensor_tensor(y_out, y0, q, ALU.mult).then_inc(step, 1)
            dve.wait_ge(step, turn * 4 + 4)
            nc.vector.scalar_tensor_tensor(nb_out, mean, -1.0, y_out, ALU.mult, ALU.mult).then_inc(done, 1)

        @block.sync
        def _(sp):
            sp.dma_start(w0[:], a["w0"]).then_inc(consts_in, 16)
            sp.dma_start(cols[:, 0:10], a["cols"]).then_inc(consts_in, 16)
            sp.dma_start(xs[:, 0], xin[:, 0:NT, :]).then_inc(A0["x_in"][0], 16)
            adj_v = a["adj"].rearrange("(t p) m -> p t m", p=P)
            adjt_v = a["adjt"].rearrange("(t p) m -> p t m", p=P)
            stage = X[:].rearrange("p b t c -> p b (t c)")
            for i in range(4):
                sp.dma_start(stage[:, 2 * i:2 * i + 2, :], adj_v[:, 2 * i:2 * i + 2, :]).then_inc(g_in[i], 16)
            for dst, name in ((w3, "w3"), (w3t, "w3t"), (w1t, "w1t"), (acol, "acol")):
                sp.dma_start(dst[:], a[name]).then_inc(consts_in, 16)
            sp.dma_start(w2t[:], a["w2t"].rearrange("(h p) o -> p h o", p=P)).then_inc(consts_in, 16)
            sp.dma_start(wl2[:], a["wl2"].rearrange("k p o -> p k o")).then_inc(consts_in, 16)
            for dst, name in ((bias0, "b"), (bias0b, "b_lin"), (bias2, "bias2")):
                sp.dma_start(dst[:], a[name].broadcast_to([P, C])).then_inc(consts_in, 16)
            for i in range(4):
                sp.wait_ge(g_cast, 2 * i + 2)
                sp.dma_start(stage[:, 2 * i:2 * i + 2, :], adjt_v[:, 2 * i:2 * i + 2, :]).then_inc(at_in[i], 16)

            def l0(k):
                if k.nxt and k.index != -1:
                    if k.prev:
                        sp.wait_ge(A0["xt_ps"], k.b * 2)
                        sp.wait_ge(A0["xb_ok"], k.b)
                    sp.dma_start(xs[:, 1 - k.p], xin[:, bass.ds((k.b + 1) * NT, NT), :]).then_inc(
                        A0["x_in"][1 - k.p], 16)

            for_batches(sp, B, l0)

            def l3(k):
                if k.nxt:
                    sp.wait_ge(e_x, k.b + 2)
                    alone(sp)
                    if k.prev:
                        sp.wait_ge(A3["xt_ps"], k.b * 2)
                    alone(sp)
                    sp.dma_start(xs[:, 1 - k.p].rearrange("p t c -> p (t c)"), xall(k.b + 1)).then_inc(
                        A3["x_in"][1 - k.p], 16)

            for_batches(sp, B, l3)
            for h in range(2):
                sp.wait_ge(A3["out_ok"][h], 16 * (B + 1))

        @block.gpsimd
        def _(pool):
            nc.gpsimd.memset(U[:, 0, 0:P], 1.0).then_inc(setup_ok, 1)
            nc.gpsimd.memset(epsc[:], EPS).then_inc(setup_ok, 1)
            pool.wait_ge(setup_ok, 1)
            nc.gpsimd.affine_select(out=ident[:], in_=U[:, 0, 0:P], compare_op=EQ, fill=0.0, base=0,
                                    pattern=[[-1, P]], channel_multiplier=1).then_inc(ident_ok, 1)
            pool.wait_ge(ident_ok, 1)
            for t in range(NT):
                pool.wait_ge(at_in[t // 2], 16)
                blk = X[:, t, t, :]
                nc.gpsimd.affine_select(out=DU[:, t, :], in_=blk, compare_op=ALU.is_gt, fill=0.0, base=0,
                                        pattern=[[-1, P]], channel_multiplier=1).then_inc(tri_ok, 1)
                nc.gpsimd.affine_select(out=DL[:, t, :], in_=blk, compare_op=ALU.is_gt, fill=0.0, base=0,
                                        pattern=[[1, P]], channel_multiplier=-1).then_inc(tri_ok, 1)
                nc.gpsimd.affine_select(out=DD[:, t, :], in_=blk, compare_op=EQ, fill=0.0, base=0,
                                        pattern=[[-1, P]], channel_multiplier=1).then_inc(tri_ok, 1)
                pool.wait_ge(at_cast, t + 1)
                dblk = AT[:, t, t * P:(t + 1) * P]
                nc.gpsimd.tensor_tensor(dblk, dblk.bitcast(F32), ident[:], ALU.add).then_inc(tri_ok, 1)

            def l0(k):
                if k.index == -1:
                    return
                if k.index == 0:
                    pool.wait_ge(tri_ok, 4 * NT)
                    pool.wait_ge(bias0_ok, 1)
                    pool.wait_ge(at_cast, NT)
                for bb, par in ([(0, 0)] if k.index == 0 else []) + ([(k.b + 1, 1 - k.p)] if k.nxt else []):
                    pool.wait_ge(A0["xt_ps"], bb * 2 + 2)
                    nc.gpsimd.tensor_tensor(v4(xall(bb)), xs[:, par], bias0b[:].unsqueeze(1).broadcast_to([P, NT, C]),
                                            ALU.add).then_inc(A0["xb_ok"], 1)

            for_batches(pool, B, l0)

            def l2(k):
                if k.nxt:
                    pool.wait_ge(c_x, k.b + 2)
                    if k.prev:
                        pool.wait_ge(e_bn, k.b * NT)
                        pool.wait_ge(e_x, k.b)
                    nc.gpsimd.tensor_tensor(xb2[:, 1 - k.p], v4(xall(k.b + 1)),
                                            bias2[:].unsqueeze(1).broadcast_to([P, NT, C]), ALU.add).then_inc(e_xb, 1)

            for_batches(pool, B, l2)

            def l3(k):
                if not k.cur:
                    return
                for r in range(NT):
                    s = k.b * NT + r
                    pool.wait_ge(A3["mask_done"], s + 1)
                    if k.prev or r >= 2:
                        pool.wait_ge(A3["w_done"], s - 1)
                    alone(pool)
                    nc.gpsimd.tensor_scalar(U[:, r % 2, :], T[:, r % 4, :], 0.2, scol[:, k.p, r, 1:2],
                                            ALU.mult, ALU.add).then_inc(A3["u_ok"], 1)

            for_batches(pool, B, l3)

        @block.tensor
        def _(pe):
            pe.wait_ge(consts_in, 16 * NCONST)
            pe.wait_ge(ident_ok, 1)
            nc.tensor.matmul(psO[:, 0:2], w3t[:], acol[:], start=True, stop=True).then_inc(wa_ps, 1)
            att_pe(pe, 0, A0)

            pe.wait_ge(dinv_ok, 1)
            for t in range(NT):
                tr = nc.tensor.transpose(psS[0][:, t * P:(t + 1) * P], dinv[:, t:t + 1].broadcast_to([P, P]), ident[:])
            tr.then_inc(db_ps, 1)

            zbanks = (psT[0], psT[1], psO, psB)

            def l1a(k):
                b, p = k.b, k.p
                if k.cur:
                    pe.wait_ge(alo_ok, b + 1)
                    if k.index == 0:
                        pe.wait_ge(tri_ok, 4 * NT)
                    if k.prev:
                        pe.wait_ge(ag_ok, b)
                    for q in range(2):
                        for m in range(NT):
                            for part in range(2):
                                mm = nc.tensor.matmul(psS[p][:, q * HN:(q + 1) * HN], FR[:, p, part, m * P:(m + 1) * P],
                                                      AT[:, m, q * HN:(q + 1) * HN], start=(m == 0 and part == 0),
                                                      stop=(m == NT - 1 and part == 1))
                    mm.then_inc(ag_ps, 1)
                if k.prev:
                    pe.wait_ge(ag_ok, b + 1)
                    pe.wait_ge(z_ok, b * 4)
                    for i in range(4):
                        h, q = i // 2, i % 2
                        nc.tensor.matmul(zbanks[i][:], w1t[:, h * P:(h + 1) * P], agS[:, 1 - p, q * HN:(q + 1) * HN],
                                         start=True, stop=True).then_inc(z_ps, 1)

            for_batches(pe, B, l1a)

            def l1b(k):
                if not k.cur:
                    return
                b, p = k.b, k.p
                pe.wait_ge(relu_ok, b * 2 + 2)
                if k.prev:
                    pe.wait_ge(z2_ok, b)
                for q in range(2):
                    for h in range(HB):
                        mm = nc.tensor.matmul(psS[p][:, q * HN:(q + 1) * HN], w2t[:, h, :],
                                              zrow(h, b, q * HN, HN), start=(h == 0), stop=(h == HB - 1))
                mm.then_inc(z2_ps, 1)

            for_batches(pe, B, l1b)

            def adj_part(p, banks, diag, ranges, upper):
                for q in range(2):
                    first = True
                    for m in (range(NT - 1, -1, -1) if upper else range(NT)):
                        c0, c1 = ranges(m, q)
                        for part in range(2):
                            x_m = FR[:, p, part, m * P:(m + 1) * P]
                            if c1 > c0:
                                mm = nc.tensor.matmul(banks(c0, c1), x_m, AT[:, m, c0:c1], start=first, stop=True,
                                                      skip_group_check=True)
                                first = False
                        for part in range(2):
                            x_m = FR[:, p, part, m * P:(m + 1) * P]
                            if m // HT == q:
                                mm = nc.tensor.matmul(banks(m * P, (m + 1) * P), x_m, diag[:, m, :], start=first,
                                                      stop=True, skip_group_check=True)
                                first = False
                mm.then_inc(e_ps, 1)

            def psd(c0, c1):
                return psT[c0 // HN][:, c0 % HN:c0 % HN + c1 - c0]

            def l2(k):
                b, p = k.b, k.p
                if k.nxt:
                    pe.wait_ge(zn_ok, b + 2)
                    if k.prev:
                        pe.wait_ge(e_y, b * 2)
                    for t in range(NT):
                        tr = nc.tensor.transpose((psO if t < HT else psB)[:, t % HT * P:(t % HT + 1) * P],
                                                 zn[:, t * P:(t + 1) * P], ident[:])
                    tr.then_inc(c_ps, 1)
                if k.cur:
                    pe.wait_ge(e_lo, b + 1)
                    if k.prev:
                        pe.wait_ge(e_ok, b * 3 - 2)
                    adj_part(p, lambda c0, c1: psS[0][:, c0:c1], DU,
                             lambda m, q: (q * HN, min(m * P, (q + 1) * HN)), True)
                if k.prev:
                    pe.wait_ge(e_ok, b * 3)
                    if k.nxt:
                        pe.wait_ge(c_y, b * 2 + 4)
                    elif k.index == B:
                        pe.wait_ge(e_y, b * 2)
                    for t in range(NT):
                        for j, w in enumerate((1, 2, 0)):
                            mm = nc.tensor.matmul((psO if t < HT else psB)[:, t % HT * P:(t % HT + 1) * P],
                                                  UDL[:, 1 - p, j, t * P:(t + 1) * P], wl2[:, w, :],
                                                  start=(j == 0), stop=(j == 2))
                    mm.then_inc(e_out, 1)
                if k.cur:
                    if k.prev:
                        pe.wait_ge(e_ok, b * 3)
                    adj_part(p, lambda c0, c1: psS[1][:, c0:c1], DL,
                             lambda m, q: (max((m + 1) * P, q * HN), (q + 1) * HN), False)
                    adj_part(p, psd, DD, lambda m, q: (0, 0), False)

            for_batches(pe, B, l2)
            pe.wait_ge(e_y, 2 * B + 2)
            att_pe(pe, 3, A3)

        @block.scalar
        def _(act):
            act.preload_act_table_set("natural_log_exp_and_others")
            for t in range(NT):
                act.wait_ge(g_in[t // 2], 16)
                nc.scalar.activation(G[:, t, :], X[:, t].rearrange("p t c -> p (t c)"), ACT.Copy, scale=-1.0,
                                     accum_out=deg[:, 0, t:t + 1]).then_inc(g_cast, 1)
            act.wait_ge(consts_in, 16 * NCONST)
            att_act(act, 0, A0)

            def ln_exp(src, tmp, bias, l, l_value, done):
                nc.scalar.activation(tmp[:, 0], src, ACT.Ln, bias=bias).then_inc(l, 1)
                act.wait_ge(l, l_value)
                nc.scalar.activation(tmp[:, 1], tmp[:, 0], ACT.Exp, scale=-0.5).then_inc(done, 1)

            act.wait_ge(dg_ok, 2)
            ln_exp(deg[:, 3, :], newt[:, 0], 0.0, dg_l, 1, dg_ln)
            zbanks = (psT[0], psT[1], psO, psB)
            act.sem_inc(z_ok, 4)
            act.sem_inc(z2_ok, 1)

            def l1a(k):
                b, p = k.b, k.p
                if k.nxt:
                    act.wait_ge(xsc_ok, b + 2)
                    if k.prev:
                        act.wait_ge(ag_ps, b)
                    nc.scalar.copy(FR[:, 1 - p, 0, :], xsc[:, 1 - p].rearrange("p t c -> p (t c)")).then_inc(ahi_ok, 1)
                if k.prev:
                    for i in range(4):
                        h, q = i // 2, i % 2
                        act.wait_ge(z_ps, b * 4 - 3 + i)
                        alone(act)
                        nc.scalar.activation(zrow(h, b - 1, q * HN, HN), zbanks[i][:], ACT.Identity,
                                             bias=b1c[:, h:h + 1]).then_inc(z_ok, 1)

            for_batches(act, B, l1a)
            act.wait_ge(bn1_mv, 1)
            ln_exp(bnmv[:, :, 1], newt[:, 0, :, 0:HB], epsc[:], bn1_l, 1, bn1_ln)
            act.wait_ge(bn1_ok, 2)

            def l1b(k):
                b, p = k.b, k.p
                if k.nxt:
                    for h in range(HB):
                        nc.scalar.activation(zrow(h, b + 1, 0, N), zrow(h, b + 1, 0, N), ACT.Relu,
                                             bias=bnsc[:, 1, h:h + 1], scale=bnsc[:, 0, h:h + 1]).then_inc(relu_ok, 1)
                if k.cur:
                    act.wait_ge(z2_ps, b + 1)
                    alone(act)
                    nc.scalar.activation(zrow(0, b, 0, N), psS[p][:], ACT.Identity, bias=b2c).then_inc(z2_ok, 1)

            for_batches(act, B, l1b)
            act.wait_ge(bn2_mv, 1)
            ln_exp(bnmv[:, 0:1, 1], newt[:, 0, :, 0:1], epsc[:], bn2_l, 1, bn2_ln)

            def norm(b, src, i, done):
                for t in range(NT):
                    n = nc.scalar.activation(xrow(b, t), src[:, t, :], ACT.Identity, bias=nbias[:, i, t:t + 1],
                                             scale=rstd[:, i, t:t + 1])
                n.then_inc(done, 1)

            def l2(k):
                b, p = k.b, k.p
                if k.nxt:
                    act.wait_ge(c_mv, b + 2)
                    ln_exp(mv[:, 0, :, 1], newt[:, 0], epsc[:], c_l, b + 2, c_ln)
                    act.wait_ge(c_nw, b + 2)
                    alone(act)
                    norm(b + 1, Yc, 0, c_x)
                    act.wait_ge(c_x, b + 2)
                    if k.cur:
                        act.wait_ge(e_ps, b * 3) if k.prev else None
                    alone(act)
                    nc.scalar.copy(FR[:, 1 - p, 0, :], xall(b + 1)).then_inc(e_hi, 1)
                if k.cur:
                    act.wait_ge(e_ps, b * 3 + 1)
                    nc.scalar.copy(UDL[:, p, 0, :], psS[0][:]).then_inc(e_ok, 1)
                if k.prev:
                    act.wait_ge(e_mv, b)
                    ln_exp(mv[:, 1, :, 1], newt[:, 1], epsc[:], e_l, b, e_ln)
                if k.cur:
                    act.wait_ge(e_ps, b * 3 + 2)
                    nc.scalar.copy(UDL[:, p, 1, :], psS[1][:]).then_inc(e_ok, 1)
                    act.wait_ge(e_ps, b * 3 + 3)
                    for q in range(2):
                        n = nc.scalar.copy(UDL[:, p, 2, q * HN:(q + 1) * HN], psT[q][:])
                    n.then_inc(e_ok, 1)
                if k.prev:
                    act.wait_ge(e_nw, b)
                    alone(act)
                    norm(b - 1, xb2[:, 1 - p], 1, e_x)

            for_batches(act, B, l2)
            att_act(act, 3, A3)

        @block.vector
        def _(dve):
            dve.wait_ge(consts_in, 16 * NCONST)
            nc.vector.tensor_tensor(bias0b[:], bias0b[:], bias0[:], ALU.add).then_inc(bias0_ok, 1)
            dve.wait_ge(wa_ps, 1)
            for col, src, scale in ((0, 0, -1.0), (1, 0, -0.2), (2, 1, -1.0), (3, 1, -0.2)):
                nc.vector.tensor_scalar(wa[:, col:col + 1], psO[:, src:src + 1], scale, None,
                                        ALU.mult).then_inc(wa_ok, 1)
            att_dve(dve, 0, A0)

            for t in range(NT):
                nc.vector.tensor_tensor_reduce(xsc[:, 0, t, :], G[:, t, t * P:(t + 1) * P], ident[:], 1.0, 0.0,
                                               ALU.mult, ALU.add, deg[:, 2, t:t + 1]).then_inc(diag_ok, 1)
            dve.wait_ge(diag_ok, NT)
            dve.wait_ge(at_cast, NT)
            nc.vector.scalar_tensor_tensor(deg[:, 3, :], deg[:, 2, :], 1.0, deg[:, 1, :], ALU.add,
                                           ALU.add).then_inc(dg_ok, 1)
            dve.wait_ge(dg_ok, 1)
            nc.vector.tensor_tensor(deg[:, 3, :], deg[:, 3, :], deg[:, 0, :], ALU.subtract).then_inc(dg_ok, 1)
            dve.wait_ge(dg_ln, 1)
            refine(dve, deg[:, 3, :], deg[:, 3, :], newt[:, 0], dinv[:], small[:, 0, :], dg_step, 0, dinv_ok, 0.0)
            dve.wait_ge(db_ps, 1)
            nc.vector.tensor_copy(dinvb[:], psS[0][:]).then_inc(dinvb_ok, 1)
            dve.wait_ge(dinvb_ok, 1)
            for t in range(NT):
                nc.vector.tensor_scalar(G[:, t, :], G[:, t, :], 0.0, BIG, EQ, ALU.mult).then_inc(g3_ok, 1)
            dve.sem_inc(ag_ok, 1)
            dve.sem_inc(e_y, 2)

            def l1a(k):
                b, p = k.b, k.p
                if k.prev:
                    dve.wait_ge(ag_ps, b)
                    nc.vector.tensor_tensor(agS[:, 1 - p, :], psS[1 - p][:], dinvb[:], ALU.mult).then_inc(ag_ok, 1)
                if k.nxt:
                    dve.wait_ge(A0["norm_done"], b * 2 + 4)
                    nc.vector.tensor_tensor(xsc[:, 1 - p], v4(xall(b + 1)), dinv[:].unsqueeze(2).broadcast_to([P, NT, C]),
                                            ALU.mult).then_inc(xsc_ok, 1)
                    dve.wait_ge(xsc_ok, b + 2)
                    dve.wait_ge(ahi_ok, b + 2)
                    nc.vector.tensor_tensor(FR[:, 1 - p, 1, :], xsc[:, 1 - p].rearrange("p t c -> p (t c)"),
                                            FR[:, 1 - p, 0, :].bitcast(F32), ALU.subtract).then_inc(alo_ok, 1)
                if k.prev:
                    for i in range(4):
                        h, q = i // 2, i % 2
                        dve.wait_ge(z_ok, b * 4 + 1 + i)
                        nc.vector.bn_stats(bnst2[:, bass.ds((b - 1) * 12 + h * 12 * B + q * 6, 6)],
                                           zrow(h, b - 1, q * HN, HN)).then_inc(zst_ok, 1)

            for_batches(dve, B, l1a)

            def bn_affine(n, gamma, beta, mv_done, ln_done, step, nw, ok, i):
                for h in range(n):
                    m = nc.vector.bn_aggr(bnmv[:, h, :], bnst[:, h].rearrange("p a b -> p (a b)"))
                m.then_inc(mv_done, 1)
                dve.wait_ge(mv_done, 1)
                dve.wait_ge(ln_done, 1)
                refine(dve, bnmv[:, 0:n, 1], bnmv[:, 0:n, 0], newt[:, 0, :, 0:n], bnsc[:, 4, 0:n], bnsc[:, 5, 0:n],
                       step, 0, nw, EPS)
                dve.wait_ge(nw, 1)
                nc.vector.tensor_tensor(bnsc[:, i, 0:n], bnsc[:, 4, 0:n], gamma, ALU.mult).then_inc(ok, 1)
                nc.vector.tensor_tensor(bnsc[:, i + 1, 0:n], bnsc[:, 5, 0:n], gamma, ALU.mult).then_inc(nw, 1)
                dve.wait_ge(nw, 2)
                nc.vector.tensor_tensor(bnsc[:, i + 1, 0:n], bnsc[:, i + 1, 0:n], beta, ALU.add).then_inc(ok, 1)

            dve.wait_ge(zst_ok, 4 * B)
            bn_affine(HB, g1c, be1c, bn1_mv, bn1_ln, bn1_step, bn1_nw, bn1_ok, 0)

            def l1b(k):
                if not k.cur:
                    return
                dve.wait_ge(z2_ok, k.b + 2)
                for q in range(2):
                    nc.vector.bn_stats(bnst2[:, bass.ds(k.b * 12 + q * 6, 6)],
                                       zrow(0, k.b, q * HN, HN)).then_inc(z2st_ok, 1)

            for_batches(dve, B, l1b)
            dve.wait_ge(z2st_ok, 2 * B)
            bn_affine(1, g2c, be2c, bn2_mv, bn2_ln, bn2_step, bn2_nw, bn2_ok, 2)
            dve.wait_ge(bn2_ok, 2)

            def l2(k):
                b, p = k.b, k.p

                def layer_stats(src, i, turn, y_sem, y_value, bn, mv_done):
                    for t in range(NT):
                        dve.wait_ge(y_sem, y_value + t // HT)
                        nc.vector.bn_stats(stats[:, i, t, :], src[:, t, :]).then_inc(bn, 1)
                    dve.wait_ge(bn, turn * NT + NT)
                    alone(dve)
                    for t in range(NT):
                        m = nc.vector.bn_aggr(mv[:, i, t, :], stats[:, i, t, :])
                    m.then_inc(mv_done, 1)

                if k.nxt:
                    if k.cur:
                        dve.wait_ge(c_ps, b + 1)
                    nc.vector.tensor_scalar(zn[:], zrow(0, b + 1, 0, N), bnsc[:, 2, 0:1], bnsc[:, 3, 0:1], ALU.mult,
                                            ALU.add).then_inc(zn_ok, 1)
                    dve.wait_ge(c_ps, b + 2)
                    if k.cur:
                        dve.wait_ge(c_x, b + 1)
                    for h in range(2):
                        nc.vector.tensor_tensor(Yc[:, h * HT:(h + 1) * HT, :].rearrange("p t c -> p (t c)"),
                                                (psO, psB)[h][:], X2[:, bass.ds((b + 1) * N + h * HN, HN)],
                                                ALU.add).then_inc(c_y, 1)
                    layer_stats(Yc, 0, b + 1, c_y, b * 2 + 3, c_bn, c_mv)
                    dve.wait_ge(c_ln, b + 2)
                    refine(dve, mv[:, 0, :, 1], mv[:, 0, :, 0], newt[:, 0], rstd[:, 0, :], nbias[:, 0, :], c_step,
                           b + 1, c_nw, EPS)
                if k.prev:
                    dve.wait_ge(e_out, b)
                    dve.wait_ge(e_xb, b)
                    y2 = xb2[:, 1 - p]
                    for h in range(2):
                        ys = y2[:, h * HT:(h + 1) * HT, :].rearrange("p t c -> p (t c)")
                        nc.vector.tensor_tensor(ys, (psO, psB)[h][:], ys, ALU.add).then_inc(e_y, 1)
                    layer_stats(y2, 1, b - 1, e_y, b * 2 + 1, e_bn, e_mv)
                if k.nxt:
                    dve.wait_ge(e_hi, b + 2)
                    nc.vector.tensor_tensor(FR[:, 1 - p, 1, :], xall(b + 1), FR[:, 1 - p, 0, :].bitcast(F32),
                                            ALU.subtract).then_inc(e_lo, 1)
                if k.prev:
                    dve.wait_ge(e_ln, b)
                    refine(dve, mv[:, 1, :, 1], mv[:, 1, :, 0], newt[:, 1], rstd[:, 1, :], nbias[:, 1, :], e_step,
                           b - 1, e_nw, EPS)

            for_batches(dve, B, l2)
            dve.wait_ge(g3_ok, NT)
            for h in range(2):
                dve.sem_inc(A3["out_ok"][h], 16)
            att_dve(dve, 3, A3)


def kernel(x, adj, L0_gnn_W, L0_gnn_b_lin, L0_gnn_b, L1_gnn_W1, L1_gnn_b1, L1_gnn_g1, L1_gnn_be1, L1_gnn_W2,
           L1_gnn_b2, L1_gnn_g2, L1_gnn_be2, L2_gnn_W, L2_gnn_bias, L3_gnn_W, L3_gnn_a):
    import numpy as np
    import concourse.bacc as bacc
    from concourse.bass_utils import run_bass_kernel_spmd

    def lay(v):
        return np.ascontiguousarray(np.asarray(v))

    cols = np.concatenate([np.asarray(v).reshape(-1, P) for v in (
        L0_gnn_b_lin, L1_gnn_b1, L1_gnn_g1, L1_gnn_be1, L1_gnn_b2, L1_gnn_g2, L1_gnn_be2)])
    arrays = {
        "x": lay(x), "adj": lay(adj), "adjt": lay(np.asarray(adj).T), "w0": lay(L0_gnn_W), "cols": lay(cols.T),
        "b": lay(np.asarray(L0_gnn_b)[None]), "b_lin": lay(np.asarray(L0_gnn_b_lin)[None]),
        "w1t": lay(np.asarray(L1_gnn_W1).T), "w2t": lay(np.asarray(L1_gnn_W2).T), "wl2": lay(L2_gnn_W),
        "bias2": lay(np.asarray(L2_gnn_bias)[None]), "w3": lay(L3_gnn_W), "w3t": lay(np.asarray(L3_gnn_W).T),
        "acol": lay(np.asarray(L3_gnn_a).reshape(2, P).T),
    }
    nc = bacc.Bacc("TRN2", target_bir_lowering=False, num_devices=1)
    aps = {n: nc.dram_tensor(f"{n}_dram", v.shape, mybir.dt.from_np(v.dtype), kind="ExternalInput").ap()
           for n, v in arrays.items()}
    out = nc.dram_tensor("out_dram", x.shape, F32, kind="ExternalOutput").ap()
    graph_layers(nc, aps, out)
    r = run_bass_kernel_spmd(nc, [{f"{n}_dram": v for n, v in arrays.items()}], core_ids=[0])
    return r.results[0]["out_dram"]
```

```python
from contextlib import ExitStack

import concourse.bass as bass
from concourse import mybir

P = 128
EPS = 1e-5
NEG = 1e16
BIG = 1e30
NCONST = 9
CLAMP = 1e20
F32, F32R, BF16 = mybir.dt.float32, mybir.dt.float32r, mybir.dt.bfloat16
ALU, ACT = mybir.AluOpType, mybir.ActivationFunctionType
EQ = ALU.is_equal


class Batch:

    def __init__(self, b, n, p, count):
        self.b, self.n, self.p = b, n, p
        known = isinstance(b, int)
        self.prev = not known or b >= 1
        self.cur = not known or 0 <= b < count
        self.nxt = not known or b < count - 1
        self.index = b if known else None


def before(eng, count, body):
    body(Batch(-1, -1, 1, count))


def batches(eng, count, body):
    body(Batch(0, 0, 0, count))
    with eng.Fori(0, (count - 2) // 2) as i:
        body(Batch(i * 2 + 1, i, 1, count))
        body(Batch(i * 2 + 2, i + 1, 0, count))
    body(Batch(count - 1, (count - 1) // 2, 1, count))


def after(eng, count, body):
    body(Batch(count, count // 2, 0, count))


def for_batches(eng, count, body):
    before(eng, count, body)
    batches(eng, count, body)
    after(eng, count, body)


def graph_layers(nc, a, out):
    B, N, C = a["x"].shape
    NT = N // P
    HT = NT // 2
    HN = N // 2
    HB = a["w1t"].shape[1] // P
    assert C == P and NT == 8 and HB == 2 and B % 2 == 0

    with ExitStack() as ctx:
        def sb(name, shape, dt=F32):
            return ctx.enter_context(nc.sbuf_tensor(name, shape, dt))

        def sem(name):
            return ctx.enter_context(nc.semaphore(name))

        X = sb("X", [P, B, NT, C])
        AT = sb("AT", [P, NT, N], F32R)
        DU = sb("DU", [P, NT, P], F32R)
        DL = sb("DL", [P, NT, P], F32R)
        DD = sb("DD", [P, NT, P], F32R)
        G = sb("G", [P, NT, N], BF16)
        FR = sb("FR", [P, 2, 2, N], F32R)
        arena = sb("arena", [P, 84 * 256])
        dinvb = sb("dinvb", [P, N])
        ident = sb("ident", [P, P])
        w0, w3 = sb("w0", [P, C]), sb("w3", [P, C])
        w1t, w2t, wl2 = sb("w1tS", [P, HB * P]), sb("w2tS", [P, HB, C]), sb("wl2S", [P, 3, C])
        w3t = sb("w3tS", [P, C])
        bias0, bias0b, bias2 = sb("bias0", [P, C]), sb("bias0b", [P, C]), sb("bias2", [P, C])
        cols = sb("cols", [P, 12])
        acol = sb("acol", [P, 2])
        wa = sb("wa", [P, 4])
        epsc = sb("epsc", [P, 1])
        negmax = sb("negmax", [P, 2 * NT])
        sums = sb("sums", [P, 2 * NT])
        rsum = sb("rsum", [P, NT])
        small = sb("small", [P, 2, NT])
        stats = sb("stats", [P, 2, NT, 6])
        mv = sb("mv", [P, 2, NT, 2])
        newt = sb("newt", [P, 2, 4, NT])
        rstd = sb("rstd", [P, 2, NT])
        nbias = sb("nbias", [P, 2, NT])
        deg = sb("deg", [P, 4, NT])
        dinv, dtmp = sb("dinv", [P, NT]), sb("dtmp", [P, 4, NT])
        bnst = sb("bnst", [P, HB, 2 * B, 6])
        bnmv = sb("bnmv", [P, HB, 2])
        bnsc = sb("bnsc", [P, 6, HB])
        scol = sb("scol", [P, 2, NT, 4])

        def region(kb, size_kb):
            return arena[:, kb * 256:(kb + size_kb) * 256]

        bnst2 = bnst[:].rearrange("p h a b -> p (h a b)")
        xin = a["x"].rearrange("b (t p) c -> p (b t) c", p=P)
        outv = out.rearrange("b (t p) c -> p (b t) c", p=P)
        G2 = G[:].rearrange("p t n -> p (t n)")
        X2 = X[:].rearrange("p b t c -> p (b t c)")
        xs = region(0, 8).rearrange("p (q t c) -> p q t c", q=2, c=C)
        xT = region(8, 4)
        hN = region(12, 8).rearrange("p (q t c) -> p q t c", q=2, c=C)
        T = region(20, 16).rearrange("p (q n) -> p q n", q=4)
        U = region(36, 8).rearrange("p (q n) -> p q n", q=2)
        PT = region(44, 32).rearrange("p (q m n) -> p q m n", q=2, m=NT)
        OT = region(76, 4).rearrange("p (q n) -> p q n", q=2)
        Y = region(80, 4).rearrange("p (q t c) -> p q t c", q=2, c=C)
        Z1 = region(0, 64).rearrange("p (h n) -> p h n", h=HB)
        Z1f = region(0, 64)
        agS = region(72, 8).rearrange("p (q n) -> p q n", q=2)
        UDL = region(32, 24).rearrange("p (q k n) -> p q k n", q=2, k=3)
        zn = region(56, 4)
        diag_tmp = dinvb[:].rearrange("p (t c) -> p t c", c=C)
        Yc = region(60, 4).rearrange("p (t c) -> p t c", c=C)
        xb2 = region(64, 8).rearrange("p (q t c) -> p q t c", q=2, c=C)

        blin, b1c, g1c, be1c, b2c, g2c, be2c = (
            cols[:, 0:1], cols[:, 1:3], cols[:, 3:5], cols[:, 5:7], cols[:, 7:8], cols[:, 8:9], cols[:, 9:10])

        def ps(name, shape):
            return ctx.enter_context(nc.psum_tensor(name, shape, F32))

        psS = [ps("psS0", [P, N]), ps("psS1", [P, N])]
        psT = [ps("psT0", [P, HN]), ps("psT1", [P, HN])]
        psO, psB = ps("psO", [P, HN]), ps("psB", [P, HN])

        consts_in, ident_ok, setup_ok, g_cast, at_cast, tri_ok, bias0_ok, wa_ps, wa_ok, g3_ok = (
            sem(n) for n in ("consts_in", "ident_ok", "setup_ok", "g_cast", "at_cast", "tri_ok", "bias0_ok",
                             "wa_ps", "wa_ok", "g3_ok"))
        g_in = [sem(f"g_in{i}") for i in range(4)]
        at_in = [sem(f"at_in{i}") for i in range(4)]
        gate, w0_in = sem("gate"), sem("w0_in")
        diag_ok, dg_ok, dg_l, dg_ln, dg_step, dinv_ok, db_ps, dinvb_ok = (
            sem(n) for n in ("diag_ok", "dg_ok", "dg_l", "dg_ln", "dg_step", "dinv_ok", "db_ps", "dinvb_ok"))
        (ahi_ok, alo_ok, ag_ps, ag_ok, z_ps, z_ok, zst_ok, bn1_mv, bn1_l, bn1_ln, bn1_step, bn1_nw, bn1_ok,
         relu_ok, z2_ps, z2_ok, z2st_ok, bn2_mv, bn2_l, bn2_ln, bn2_step, bn2_nw, bn2_ok) = (
            sem(n) for n in ("ahi_ok alo_ok ag_ps ag_ok z_ps z_ok zst_ok bn1_mv bn1_l bn1_ln bn1_step bn1_nw "
                             "bn1_ok relu_ok z2_ps z2_ok z2st_ok bn2_mv bn2_l bn2_ln bn2_step bn2_nw bn2_ok").split())
        (zn_ok, c_ps, c_y, c_bn, c_mv, c_l, c_ln, c_step, c_nw, c_x, e_hi, e_lo, e_xb, e_ps, e_ok, e_out, e_y,
         e_bn, e_mv, e_l, e_ln, e_step, e_nw, e_x) = (
            sem(n) for n in ("zn_ok c_ps c_y c_bn c_mv c_l c_ln c_step c_nw c_x e_hi e_lo e_xb e_ps e_ok e_out e_y "
                             "e_bn e_mv e_l e_ln e_step e_nw e_x").split())

        def att_semaphores(tag):
            names = ("scores_done mask_done zero_done w_done exp_done tr_done pt_done pv_done ot_done back_done "
                     "bn_done lnexp_done newt_done norm_done xt_ps xt_ok ht_ps hi_ok lo_ok hn_ps hn_ok xb_ok u_ok "
                     "s_ps s_ok sb_ps nm_ok rs_ok mv_ok l_ok newt_step y0_ok").split()
            sems = {n: sem(f"{tag}_{n}") for n in names}
            sems["x_in"] = [sem(f"{tag}_x_in{i}") for i in range(2)]
            sems["out_ok"] = [sem(f"{tag}_out_ok{i}") for i in range(2)]
            return sems

        A0, A3 = att_semaphores("l0"), att_semaphores("l3")

        block = ctx.enter_context(nc.Block())

        def v4(t):
            return t.rearrange("p (t c) -> p t c", c=C)

        def xrow(b, t):
            return X2[:, bass.ds(b * N + t * C, C)]

        def zrow(h, b, c0, n):
            return Z1f[:, bass.ds(b * N + (h * B * N + c0), n)]

        def xall(b):
            return X2[:, bass.ds(b * N, N)]

        def alone(eng):
            eng.sem_inc(gate, 1)


        Y_AT = {0: (2, 6), 3: (4, 7)}
        LN_EXP_AT = {0: (3, 6), 3: (3, 7)}
        REFINE_AT = {0: (5, 7), 3: (6, 7)}
        NORM_AT = {0: (5, 7), 3: (5, 7)}

        def att_pe(pe, L, A):
            w_val = w0 if L == 0 else w3

            def scores(q, r, s):
                hi, lo = FR[:, q, 0], FR[:, q, 1]
                cs = slice(r * P, (r + 1) * P)
                for ch in range(2):
                    o = psS[r % 2][:, ch * HN:(ch + 1) * HN]
                    cc = slice(ch * HN, (ch + 1) * HN)
                    nc.tensor.matmul(o, hi[:, cs], hi[:, cc], start=True, stop=False)
                    nc.tensor.matmul(o, hi[:, cs], lo[:, cc], start=False, stop=False)
                    mm = nc.tensor.matmul(o, lo[:, cs], hi[:, cc], start=False, stop=True)
                mm.then_inc(A["scores_done"], 1)

            def body(k):
                b, p = k.b, k.p
                for r in range(NT):
                    s = b * NT + r
                    if L == 0 and k.index == B and r == 1:
                        pe.wait_ge(dinv_ok, 1)
                        for t in range(NT):
                            tr = nc.tensor.transpose(psS[0][:, t * P:(t + 1) * P],
                                                     dinv[:, t:t + 1].broadcast_to([P, P]), ident[:])
                        tr.then_inc(db_ps, 1)
                    if L == 0 and (k.cur if r < NT - 1 else k.nxt):
                        if r == NT - 1:
                            pe.wait_ge(A["lo_ok"], b * 2 + 4)
                        if k.prev or (k.cur and r >= 1):
                            pe.wait_ge(A["mask_done"], s)
                        if r < NT - 1:
                            scores(p, r + 1, s + 1)
                        else:
                            scores(1 - p, 0, s + 1)
                    if k.prev and r == 0 or k.cur and r >= 1:
                        tile = (r - 1) % NT
                        pe.wait_ge(A["exp_done"], s)
                        for half in range(2):
                            if k.prev or r >= 2:
                                pe.wait_ge(A["pt_done"], s * 2 - 3 + half)
                            for m in range(HT):
                                blk = half * HT + m
                                tr = nc.tensor.transpose(psT[half][:, m * P:(m + 1) * P],
                                                         T[:, tile % 4, blk * P:(blk + 1) * P], ident[:])
                            tr.then_inc(A["tr_done"], 1)
                    if (k.prev and r <= 4) or (k.cur and r >= 5):
                        j = (r - 1) % 4
                        if j == 0:
                            half_no = b * 2 + (r - 1) // 4 - 1
                            pe.wait_ge(A["pt_done"], b * 16 + (r - 1) * 2)
                            if k.prev:
                                pe.wait_ge(A["ot_done"], half_no)
                            if r == 5:
                                pe.wait_ge(A["hn_ok"], b * 2 + 2)
                        q = p if r >= 5 else 1 - p
                        hq = (((r - 1) // 4) - 1) % 2
                        for m in (2 * j, 2 * j + 1):
                            mm = nc.tensor.matmul(psO[:], hN[:, q, m, :], PT[:, hq, m, :],
                                                  start=(m == 0), stop=(m == NT - 1))
                        if j == 3:
                            mm.then_inc(A["pv_done"], 1)
                    if r in (1, 5) and k.prev:
                        half_no = b * 2 - 2 + r // 4
                        pe.wait_ge(A["ot_done"], half_no + 1)
                        if r == 1 and k.nxt:
                            pe.wait_ge(A["xt_ok"], b * 2 + 3)
                        elif r == 1 and k.index == B - 1:
                            pe.wait_ge(A["hn_ok"], B * 2)
                        elif k.nxt:
                            pe.wait_ge(A["lo_ok"] if L == 0 else A["s_ok"], b * 2 + 4 if L == 0 else b + 2)
                        else:
                            pe.wait_ge(A["y0_ok"], half_no)
                        for t in range(HT):
                            tr = nc.tensor.transpose(psB[:, t * P:(t + 1) * P],
                                                     OT[:, r // 4, t * P:(t + 1) * P], ident[:])
                        tr.then_inc(A["back_done"], 1)
                    if not k.nxt:
                        continue
                    if r in (0, 2):
                        if r == 0:
                            pe.wait_ge(A["x_in"][1 - p], (k.n + (1 if p else 0)) * 16 + 16)
                            if k.cur:
                                pe.wait_ge(A["hn_ok"], b * 2 + 2)
                        elif k.prev:
                            pe.wait_ge(A["y0_ok"], b * 2 - 1)
                        elif r == 2:
                            pe.wait_ge(A["xt_ok"], b * 2 + 3)
                        for t in range(HT):
                            tr = nc.tensor.transpose(psB[:, t * P:(t + 1) * P],
                                                     xs[:, 1 - p, r // 2 * HT + t, :], ident[:])
                        tr.then_inc(A["xt_ps"], 1)
                    if L == 0 and r in (3, 4):
                        if k.index == -1:
                            pe.wait_ge(w0_in, 32)
                        if r == 3:
                            pe.wait_ge(A["xt_ok"], b * 2 + 4)
                        else:
                            pe.wait_ge(A["lo_ok"], b * 2 + 3)
                        nc.tensor.matmul(psB[:], w0[:], xT[:, (r - 3) * HN:(r - 2) * HN],
                                         start=True, stop=True).then_inc(A["ht_ps"], 1)
                    if L == 3 and r == 3:
                        pe.wait_ge(A["xt_ok"], b * 2 + 4)
                        for t in range(NT):
                            mm = nc.tensor.matmul(psB[:, t * 4:t * 4 + 4], xT[:, t * P:(t + 1) * P], wa[:],
                                                  start=True, stop=True)
                        mm.then_inc(A["s_ps"], 1)
                    if L == 3 and r == 4:
                        pe.wait_ge(A["s_ok"], b + 2)
                        if k.prev:
                            pe.wait_ge(A["mask_done"], b * NT)
                        for t in range(NT):
                            tr = nc.tensor.transpose(psS[1 - p][:, t * P:(t + 1) * P],
                                                     scol[:, 1 - p, t, 2:3].broadcast_to([P, P]), ident[:])
                        tr.then_inc(A["sb_ps"], 1)
                    if r in (6, 7):
                        if r == 7:
                            pe.wait_ge(A["hn_ok"], b * 2 + 3)
                        elif k.prev:
                            pe.wait_ge(A["y0_ok"], b * 2)
                        else:
                            pe.wait_ge(A["lo_ok"] if L == 0 else A["s_ok"], b * 2 + 4 if L == 0 else b + 2)
                        for t in range(HT):
                            tt = (r - 6) * HT + t
                            mm = nc.tensor.matmul(psB[:, t * P:(t + 1) * P], xT[:, tt * P:(tt + 1) * P],
                                                  w_val[:], start=True, stop=True)
                        mm.then_inc(A["hn_ps"], 1)

            return body

        def att_act(act, L, A):
            def aux(b, p, r, cur):
                if r in (0, 2):
                    act.wait_ge(A["xt_ps"], b * 2 + 3 + r // 2)
                    if r == 0 and cur:
                        act.wait_ge(A["hn_ps"], b * 2 + 2)
                    nc.scalar.copy(xT[:, r // 2 * HN:(r // 2 + 1) * HN], psB[:]).then_inc(A["xt_ok"], 1)
                if L == 0 and r in (3, 4):
                    act.wait_ge(A["ht_ps"], b * 2 + r)
                    nc.scalar.activation(FR[:, 1 - p, 0, (r - 3) * HN:(r - 2) * HN], psB[:], ACT.Identity,
                                         bias=blin).then_inc(A["hi_ok"], 1)
                if L == 3 and r == 3:
                    act.wait_ge(A["s_ps"], b + 2)
                    nc.scalar.copy(scol[:, 1 - p, :, :].rearrange("p t k -> p (t k)"),
                                   psB[:, 0:NT * 4]).then_inc(A["s_ok"], 1)
                if r in (6, 7):
                    act.wait_ge(A["hn_ps"], b * 2 + r - 3)
                    nc.scalar.copy(hN[:, 1 - p, (r - 6) * HT:(r - 5) * HT, :], v4(psB[:])).then_inc(A["hn_ok"], 1)

            def ln_exp(b, r):
                h = LN_EXP_AT[L].index(r)
                half_no = b * 2 - 2 + h
                act.wait_ge(A["mv_ok"], half_no + 1)
                nc.scalar.activation(newt[:, h, 0, 0:HT], mv[:, h, 0:HT, 1], ACT.Ln,
                                     bias=epsc[:]).then_inc(A["l_ok"], 1)
                act.wait_ge(A["l_ok"], half_no + 1)
                nc.scalar.activation(newt[:, h, 1, 0:HT], newt[:, h, 0, 0:HT], ACT.Exp,
                                     scale=-0.5).then_inc(A["lnexp_done"], 1)

            def exponentials(b, p, r):
                act.wait_ge(A["w_done"], b * NT + r + 1)
                i = p * NT + r
                nc.scalar.activation(T[:, r % 4, :], T[:, r % 4, :], ACT.Exp, bias=negmax[:, i:i + 1],
                                     scale=-1.0, accum_out=sums[:, i:i + 1]).then_inc(A["exp_done"], 1)

            def body(k):
                b, p = k.b, k.p
                for r in range(NT):
                    s = b * NT + r
                    if r >= 1 and k.nxt:
                        aux(b, p, r - 1, k.cur)
                    if r == 0 and k.cur:
                        aux(b - 1, 1 - p, NT - 1, k.prev)
                    if L == 0 and k.index == -1 and r >= 4:
                        for t in (2 * r - 8, 2 * r - 7):
                            act.wait_ge(g_in[t // 2], 16)
                            nc.scalar.activation(G[:, t, :], X[:, t].rearrange("p t c -> p (t c)"), ACT.Copy,
                                                 scale=-1.0, accum_out=deg[:, 0, t:t + 1]).then_inc(g_cast, 1)
                    if k.prev and r == 0 or k.cur and r >= 1:
                        j = (r - 1) % 4
                        hq = ((r - 1) // 4) % 2
                        if j == 0 and k.prev:
                            act.wait_ge(A["pv_done"], b * 2 + (r - 1) // 4 - 1)
                        for half in range(2):
                            act.wait_ge(A["tr_done"], s * 2 - 1 + half)
                            nc.scalar.copy(PT[:, hq, half * HT:(half + 1) * HT, j * P:(j + 1) * P],
                                           v4(psT[half][:])).then_inc(A["pt_done"], 1)
                    if L == 3 and k.prev and r in LN_EXP_AT[L]:
                        ln_exp(b, r)
                    if k.cur:
                        exponentials(b, p, r)
                    if L == 0 and k.prev and r in LN_EXP_AT[L]:
                        ln_exp(b, r)
                    if k.prev and r in (0, 4):
                        half_no = b * 2 - 2 + r // 4
                        act.wait_ge(A["pv_done"], half_no + 1)
                        nc.scalar.copy(OT[:, r // 4, :], psO[:]).then_inc(A["ot_done"], 1)
                    if k.prev and r in NORM_AT[L]:
                        h = NORM_AT[L].index(r)
                        half_no = b * 2 - 2 + h
                        act.wait_ge(A["newt_done"], half_no + 1)
                        alone(act)
                        for t in range(HT):
                            o = xrow(b - 1, h * HT + t) if L == 0 else Y[:, h, t, :]
                            n = nc.scalar.activation(o, Y[:, h, t, :], ACT.Identity, bias=nbias[:, h, t:t + 1],
                                                     scale=rstd[:, h, t:t + 1])
                        n.then_inc(A["norm_done"], 1)
                        if L == 3:
                            act.wait_ge(A["norm_done"], half_no + 1)
                            act.dma_start(outv[:, bass.ds((b - 1) * NT + h * HT, HT), :], Y[:, h]).then_inc(
                                A["out_ok"][h], 16)
                    if L == 0 and k.index == 0:
                        act.wait_ge(at_in[r // 2], 16)
                        nc.scalar.activation(AT[:, r, :], X[:, r].rearrange("p t c -> p (t c)"), ACT.Copy,
                                             accum_out=deg[:, 1, r:r + 1]).then_inc(at_cast, 1)
                    if L == 0 and k.index == B - 1 and r == 4:
                        act.wait_ge(dg_ok, 2)
                        nc.scalar.activation(dtmp[:, 0], deg[:, 3, :], ACT.Ln).then_inc(dg_l, 1)
                        act.wait_ge(dg_l, 1)
                        nc.scalar.activation(dtmp[:, 1], dtmp[:, 0], ACT.Exp, scale=-0.5).then_inc(dg_ln, 1)
                    if L == 0 and k.index == B and r == 0:
                        act.wait_ge(dinv_ok, 1)
                        scaled_hi(act, 0, 0)
                    if L == 0 and k.index == B and r == 1:
                        act.wait_ge(A0["scores_done"], B * NT)
                        scaled_hi(act, 1, 1)
            return body

        def att_dve(dve, L, A):
            def body(k):
                b, p = k.b, k.p
                for r in range(NT):
                    s = b * NT + r
                    i = p * NT + r
                    if L == 0 and k.index == B - 1 and r == 2:
                        degrees(dve)
                    if L == 0 and k.index == B - 1 and r == 6:
                        dve.wait_ge(dg_ln, 1)
                        refine(dve, deg[:, 3, :], deg[:, 3, :], dtmp, dinv[:], small[:, 0, :], dg_step, 0, dinv_ok, 0.0)
                    if L == 0 and k.index == B and r == 4:
                        scaled_lo(dve, 1, 1)
                    if L == 0 and k.index == B and r == 1:
                        dve.wait_ge(db_ps, 1)
                        nc.vector.tensor_copy(dinvb[:], psS[0][:]).then_inc(dinvb_ok, 1)
                        scaled_lo(dve, 0, 0)
                    t_now = T[:, r % 4, :]
                    if k.cur and (k.prev or r >= 4):
                        dve.wait_ge(A["tr_done"], s * 2 - 6)
                    if L == 0 and k.cur:
                        if k.index == 0:
                            dve.wait_ge(g_cast, r + 1)
                        dve.wait_ge(A["scores_done"], s + 1)
                        nc.vector.tensor_tensor(t_now, psS[r % 2][:], G[:, r, :], ALU.mult).then_inc(A["mask_done"], 1)
                        dve.wait_ge(A["mask_done"], s + 1)
                        nc.vector.tensor_scalar(U[:, r % 2, :], t_now, 0.0, NEG, EQ, ALU.mult).then_inc(A["zero_done"], 1)
                        dve.wait_ge(A["zero_done"], s + 1)
                        alone(dve)
                        nc.vector.tensor_tensor_reduce(t_now, t_now, U[:, r % 2, :], 1.0, 3e38, ALU.add, ALU.min,
                                                       negmax[:, i:i + 1]).then_inc(A["w_done"], 1)
                    if L == 3 and k.cur:
                        if r == 0:
                            dve.wait_ge(A["sb_ps"], b + 1)
                        alone(dve)
                        nc.vector.tensor_tensor_reduce(t_now, psS[p][:], G[:, r, :], 1.0, 3e38, ALU.add, ALU.min,
                                                       small[:, 0, r:r + 1]).then_inc(A["mask_done"], 1)
                    if L == 3 and (k.cur and r >= 1 or k.prev and r == 0):
                        q, rl = (p, r - 1) if r else (1 - p, NT - 1)
                        dve.wait_ge(A["u_ok"], s)
                        nc.vector.scalar_tensor_tensor(T[:, rl % 4, :], T[:, rl % 4, :], scol[:, q, rl, 0:1],
                                                       U[:, rl % 2, :], ALU.add, ALU.min).then_inc(A["w_done"], 1)
                    if L == 3 and k.cur:
                        dve.wait_ge(A["mask_done"], s + 1)
                        nc.vector.tensor_scalar(small[:, 1, r:r + 1], small[:, 0, r:r + 1], scol[:, p, r, 0:1], CLAMP,
                                                ALU.add, ALU.min).then_inc(A["zero_done"], 1)
                        dve.wait_ge(A["zero_done"], s + 1)
                        nc.vector.scalar_tensor_tensor(negmax[:, i:i + 1], small[:, 1, r:r + 1], 0.2,
                                                       small[:, 1, r:r + 1], ALU.mult, ALU.min).then_inc(A["nm_ok"], 1)
                    if L == 0 and k.nxt and r in (4, 5):
                        cs = slice((r - 4) * HN, (r - 3) * HN)
                        dve.wait_ge(A["hi_ok"], b * 2 + r - 1)
                        nc.vector.scalar_tensor_tensor(FR[:, 1 - p, 1, cs], psB[:], blin,
                                                       FR[:, 1 - p, 0, cs].bitcast(F32), ALU.add,
                                                       ALU.subtract).then_inc(A["lo_ok"], 1)
                    if k.prev and r == 1:
                        dve.wait_ge(A["exp_done"], b * NT)
                        nc.vector.reciprocal(rsum[:], sums[:, (1 - p) * NT:(2 - p) * NT]).then_inc(A["rs_ok"], 1)
                    if k.prev and r in Y_AT[L]:
                        h = Y_AT[L].index(r)
                        half_no = b * 2 - 2 + h
                        dve.wait_ge(A["back_done"], half_no + 1)
                        if h == 0:
                            dve.wait_ge(A["rs_ok"], b)
                            if L == 0:
                                dve.wait_ge(A["xb_ok"], b)
                        if L == 3:
                            dve.wait_ge(A["out_ok"][h], b * 16)
                        alone(dve)
                        for t in range(HT):
                            y = nc.vector.scalar_tensor_tensor(Y[:, h, t, :], psB[:, t * P:(t + 1) * P],
                                                               rsum[:, h * HT + t:h * HT + t + 1],
                                                               xrow(b - 1, h * HT + t), ALU.mult, ALU.add)
                        y.then_inc(A["y0_ok"], 1)
                        dve.wait_ge(A["y0_ok"], half_no + 1)
                        for t in range(HT):
                            nc.vector.bn_stats(stats[:, h, t, :], Y[:, h, t, :]).then_inc(A["bn_done"], 1)
                        dve.wait_ge(A["bn_done"], half_no * HT + HT)
                        alone(dve)
                        for t in range(HT):
                            m = nc.vector.bn_aggr(mv[:, h, t, :], stats[:, h, t, :])
                        m.then_inc(A["mv_ok"], 1)
                    if k.prev and r in REFINE_AT[L]:
                        h = REFINE_AT[L].index(r)
                        half_no = b * 2 - 2 + h
                        dve.wait_ge(A["lnexp_done"], half_no + 1)
                        refine(dve, mv[:, h, 0:HT, 1], mv[:, h, 0:HT, 0], newt[:, h, :, 0:HT], rstd[:, h, 0:HT],
                               nbias[:, h, 0:HT], A["newt_step"], half_no, A["newt_done"])

            return body

        def degrees(dve):
            for t in range(NT):
                nc.vector.tensor_tensor_reduce(diag_tmp[:, t, :], G[:, t, t * P:(t + 1) * P], ident[:], 1.0, 0.0,
                                               ALU.mult, ALU.add, deg[:, 2, t:t + 1]).then_inc(diag_ok, 1)
            dve.wait_ge(diag_ok, NT)
            nc.vector.scalar_tensor_tensor(deg[:, 3, :], deg[:, 2, :], 1.0, deg[:, 1, :], ALU.add,
                                           ALU.add).then_inc(dg_ok, 1)
            dve.wait_ge(dg_ok, 1)
            nc.vector.tensor_tensor(deg[:, 3, :], deg[:, 3, :], deg[:, 0, :], ALU.subtract).then_inc(dg_ok, 1)

        def scaled_hi(act, b, p):
            act.wait_ge(A0["norm_done"], b * 2 + 2)
            alone(act)
            for t in range(NT):
                h = nc.scalar.activation(FR[:, p, 0, t * P:(t + 1) * P], xrow(b, t), ACT.Copy, scale=dinv[:, t:t + 1])
            h.then_inc(ahi_ok, 1)

        def scaled_lo(dve, b, p):
            dve.wait_ge(ahi_ok, b + 1)
            alone(dve)
            for t in range(NT):
                lo = nc.vector.scalar_tensor_tensor(FR[:, p, 1, t * P:(t + 1) * P], xrow(b, t), dinv[:, t:t + 1],
                                                    FR[:, p, 0, t * P:(t + 1) * P].bitcast(F32), ALU.mult,
                                                    ALU.subtract)
            lo.then_inc(alo_ok, 1)

        def refine(dve, var, mean, tmp, y_out, nb_out, step, turn, done, eps=EPS):
            y0, q, f = tmp[:, 1], tmp[:, 2], tmp[:, 3]
            nc.vector.tensor_tensor(q, y0, y0, ALU.mult).then_inc(step, 1)
            dve.wait_ge(step, turn * 4 + 1)
            nc.vector.scalar_tensor_tensor(f, var, eps, q, ALU.add, ALU.mult).then_inc(step, 1)
            dve.wait_ge(step, turn * 4 + 2)
            nc.vector.tensor_scalar(q, f, -0.5, 1.5, ALU.mult, ALU.add).then_inc(step, 1)
            dve.wait_ge(step, turn * 4 + 3)
            nc.vector.tensor_tensor(y_out, y0, q, ALU.mult).then_inc(step, 1)
            dve.wait_ge(step, turn * 4 + 4)
            nc.vector.scalar_tensor_tensor(nb_out, mean, -1.0, y_out, ALU.mult, ALU.mult).then_inc(done, 1)

        def out_banks(k):
            return psT if k.index == B else (psO, psB)

        @block.sync
        def _(sp):
            sp.dma_start(xs[:, 0], xin[:, 0:NT, :]).then_inc(A0["x_in"][0], 16)
            sp.dma_start(w0[:], a["w0"]).then_inc(w0_in, 16)
            sp.dma_start(cols[:, 0:10], a["cols"]).then_inc(w0_in, 16)
            adj_v = a["adj"].rearrange("(t p) m -> p t m", p=P)
            adjt_v = a["adjt"].rearrange("(t p) m -> p t m", p=P)
            stage = X[:].rearrange("p b t c -> p b (t c)")
            for i in range(4):
                sp.dma_start(stage[:, 2 * i:2 * i + 2, :], adj_v[:, 2 * i:2 * i + 2, :]).then_inc(g_in[i], 16)
            for dst, name in ((w3, "w3"), (w3t, "w3t"), (w1t, "w1t"), (acol, "acol")):
                sp.dma_start(dst[:], a[name]).then_inc(consts_in, 16)
            sp.dma_start(w2t[:], a["w2t"].rearrange("(h p) o -> p h o", p=P)).then_inc(consts_in, 16)
            sp.dma_start(wl2[:], a["wl2"].rearrange("k p o -> p k o")).then_inc(consts_in, 16)
            for dst, name in ((bias0, "b"), (bias0b, "b_lin"), (bias2, "bias2")):
                sp.dma_start(dst[:], a[name].broadcast_to([P, C])).then_inc(consts_in, 16)
            sp.dma_start(xs[:, 1], xin[:, NT:2 * NT, :]).then_inc(A0["x_in"][1], 16)
            for i in range(4):
                sp.wait_ge(g_cast, 2 * i + 2)
                sp.dma_start(stage[:, 2 * i:2 * i + 2, :], adjt_v[:, 2 * i:2 * i + 2, :]).then_inc(at_in[i], 16)

            def l0(k):
                if k.nxt and k.index not in (-1, 0):
                    sp.wait_ge(A0["xt_ps"], k.b * 2)
                    sp.wait_ge(A0["xb_ok"], k.b)
                    sp.dma_start(xs[:, 1 - k.p], xin[:, bass.ds((k.b + 1) * NT, NT), :]).then_inc(
                        A0["x_in"][1 - k.p], 16)

            for_batches(sp, B, l0)

            def l3(k):
                if k.nxt:
                    sp.wait_ge(e_x, k.b + 2)
                    alone(sp)
                    if k.prev:
                        sp.wait_ge(A3["xt_ps"], k.b * 2)
                    alone(sp)
                    sp.dma_start(xs[:, 1 - k.p].rearrange("p t c -> p (t c)"), xall(k.b + 1)).then_inc(
                        A3["x_in"][1 - k.p], 16)

            for_batches(sp, B, l3)
            for h in range(2):
                sp.wait_ge(A3["out_ok"][h], 16 * (B + 1))

        @block.gpsimd
        def _(pool):
            nc.gpsimd.memset(U[:, 0, 0:P], 1.0).then_inc(setup_ok, 1)
            nc.gpsimd.memset(epsc[:], EPS).then_inc(setup_ok, 1)
            pool.wait_ge(setup_ok, 1)
            nc.gpsimd.affine_select(out=ident[:], in_=U[:, 0, 0:P], compare_op=EQ, fill=0.0, base=0,
                                    pattern=[[-1, P]], channel_multiplier=1).then_inc(ident_ok, 1)
            pool.wait_ge(ident_ok, 1)
            for t in range(NT):
                pool.wait_ge(at_in[t // 2], 16)
                blk = X[:, t, t, :]
                nc.gpsimd.affine_select(out=DU[:, t, :], in_=blk, compare_op=ALU.is_gt, fill=0.0, base=0,
                                        pattern=[[-1, P]], channel_multiplier=1).then_inc(tri_ok, 1)
                nc.gpsimd.affine_select(out=DL[:, t, :], in_=blk, compare_op=ALU.is_gt, fill=0.0, base=0,
                                        pattern=[[1, P]], channel_multiplier=-1).then_inc(tri_ok, 1)
                nc.gpsimd.affine_select(out=DD[:, t, :], in_=blk, compare_op=EQ, fill=0.0, base=0,
                                        pattern=[[-1, P]], channel_multiplier=1).then_inc(tri_ok, 1)
                pool.wait_ge(at_cast, t + 1)
                dblk = AT[:, t, t * P:(t + 1) * P]
                nc.gpsimd.tensor_tensor(dblk, dblk.bitcast(F32), ident[:], ALU.add).then_inc(tri_ok, 1)

            pool.wait_ge(consts_in, 16 * NCONST)
            nc.gpsimd.tensor_tensor(bias0b[:], bias0b[:], bias0[:], ALU.add).then_inc(bias0_ok, 1)

            def l0(k):
                if k.index == -1:
                    return
                if k.index == 0:
                    pool.wait_ge(tri_ok, 4 * NT)
                    pool.wait_ge(bias0_ok, 1)
                    pool.wait_ge(at_cast, NT)
                for bb, par in ([(0, 0)] if k.index == 0 else []) + ([(k.b + 1, 1 - k.p)] if k.nxt else []):
                    pool.wait_ge(A0["xt_ps"], bb * 2 + 2)
                    nc.gpsimd.tensor_tensor(v4(xall(bb)), xs[:, par], bias0b[:].unsqueeze(1).broadcast_to([P, NT, C]),
                                            ALU.add).then_inc(A0["xb_ok"], 1)

            for_batches(pool, B, l0)

            def l2(k):
                if k.nxt:
                    pool.wait_ge(c_x, k.b + 2)
                    if k.prev:
                        pool.wait_ge(e_bn, k.b * NT)
                        pool.wait_ge(e_x, k.b)
                    nc.gpsimd.tensor_tensor(xb2[:, 1 - k.p], v4(xall(k.b + 1)),
                                            bias2[:].unsqueeze(1).broadcast_to([P, NT, C]), ALU.add).then_inc(e_xb, 1)

            for_batches(pool, B, l2)

            def l3(k):
                if not k.cur:
                    return
                for r in range(NT):
                    s = k.b * NT + r
                    pool.wait_ge(A3["mask_done"], s + 1)
                    if k.prev or r >= 2:
                        pool.wait_ge(A3["w_done"], s - 1)
                    alone(pool)
                    nc.gpsimd.tensor_scalar(U[:, r % 2, :], T[:, r % 4, :], 0.2, scol[:, k.p, r, 1:2],
                                            ALU.mult, ALU.add).then_inc(A3["u_ok"], 1)

            for_batches(pool, B, l3)

        @block.tensor
        def _(pe):
            pe.wait_ge(ident_ok, 1)
            for_batches(pe, B, att_pe(pe, 0, A0))
            pe.wait_ge(consts_in, 16 * NCONST)

            zbanks = (psT[0], psT[1], psO, psB)

            def l1a(k):
                b, p = k.b, k.p
                if k.cur:
                    pe.wait_ge(alo_ok, b + 1)
                    if k.index == 0:
                        pe.wait_ge(tri_ok, 4 * NT)
                    if k.prev:
                        pe.wait_ge(ag_ok, b * 2)
                    for q in range(2):
                        for m in range(NT):
                            for part in range(2):
                                mm = nc.tensor.matmul(psS[p][:, q * HN:(q + 1) * HN], FR[:, p, part, m * P:(m + 1) * P],
                                                      AT[:, m, q * HN:(q + 1) * HN], start=(m == 0 and part == 0),
                                                      stop=(m == NT - 1 and part == 1))
                        mm.then_inc(ag_ps, 1)
                if k.prev:
                    pe.wait_ge(ag_ok, b * 2 + 2)
                    pe.wait_ge(z_ok, b * 4)
                    for i in range(4):
                        h, q = i // 2, i % 2
                        nc.tensor.matmul(zbanks[i][:], w1t[:, h * P:(h + 1) * P], agS[:, 1 - p, q * HN:(q + 1) * HN],
                                         start=True, stop=True).then_inc(z_ps, 1)

            for_batches(pe, B, l1a)
            pe.wait_ge(z_ok, 4 * B + 3)
            nc.tensor.matmul(psO[:, 0:2], w3t[:], acol[:], start=True, stop=True).then_inc(wa_ps, 1)

            def l1b(k):
                if not k.cur:
                    return
                b, p = k.b, k.p
                if k.prev:
                    pe.wait_ge(z2_ok, b * 2)
                for q in range(2):
                    pe.wait_ge(relu_ok, b * 4 + q * 2 + 2)
                    for h in range(HB):
                        mm = nc.tensor.matmul(psS[p][:, q * HN:(q + 1) * HN], w2t[:, h, :],
                                              zrow(h, b, q * HN, HN), start=(h == 0), stop=(h == HB - 1))
                    mm.then_inc(z2_ps, 1)

            for_batches(pe, B, l1b)

            def adj_part(p, banks, diag, ranges, upper):
                for q in range(2):
                    first = True
                    for m in (range(NT - 1, -1, -1) if upper else range(NT)):
                        c0, c1 = ranges(m, q)
                        for part in range(2):
                            x_m = FR[:, p, part, m * P:(m + 1) * P]
                            if c1 > c0:
                                mm = nc.tensor.matmul(banks(c0, c1), x_m, AT[:, m, c0:c1], start=first, stop=True,
                                                      skip_group_check=True)
                                first = False
                        for part in range(2):
                            x_m = FR[:, p, part, m * P:(m + 1) * P]
                            if m // HT == q:
                                mm = nc.tensor.matmul(banks(m * P, (m + 1) * P), x_m, diag[:, m, :], start=first,
                                                      stop=True, skip_group_check=True)
                                first = False
                mm.then_inc(e_ps, 1)

            def psd(c0, c1):
                return psT[c0 // HN][:, c0 % HN:c0 % HN + c1 - c0]

            def l2(k):
                b, p = k.b, k.p
                if k.nxt:
                    pe.wait_ge(zn_ok, b + 2)
                    if k.prev:
                        pe.wait_ge(e_y, b * 2)
                    for t in range(NT):
                        tr = nc.tensor.transpose((psO if t < HT else psB)[:, t % HT * P:(t % HT + 1) * P],
                                                 zn[:, t * P:(t + 1) * P], ident[:])
                    tr.then_inc(c_ps, 1)
                if k.cur:
                    pe.wait_ge(e_lo, b + 1)
                    if k.prev:
                        pe.wait_ge(e_ok, b * 3 - 2)
                    adj_part(p, lambda c0, c1: psS[0][:, c0:c1], DU,
                             lambda m, q: (q * HN, min(m * P, (q + 1) * HN)), True)
                if k.prev:
                    pe.wait_ge(e_ok, b * 3)
                    if k.nxt:
                        pe.wait_ge(c_y, b * 2 + 4)
                    elif k.index == B - 1:
                        pe.wait_ge(e_y, b * 2)
                    ob = out_banks(k)
                    for t in range(NT):
                        for j, w in enumerate((1, 2, 0)):
                            mm = nc.tensor.matmul(ob[t // HT][:, t % HT * P:(t % HT + 1) * P],
                                                  UDL[:, 1 - p, j, t * P:(t + 1) * P], wl2[:, w, :],
                                                  start=(j == 0), stop=(j == 2))
                    mm.then_inc(e_out, 1)
                if k.cur:
                    if k.prev:
                        pe.wait_ge(e_ok, b * 3)
                    adj_part(p, lambda c0, c1: psS[1][:, c0:c1], DL,
                             lambda m, q: (max((m + 1) * P, q * HN), (q + 1) * HN), False)
                    adj_part(p, psd, DD, lambda m, q: (0, 0), False)

            l3 = att_pe(pe, 3, A3)
            before(pe, B, l2)
            batches(pe, B, l2)
            pe.wait_ge(e_y, 2 * B)
            pe.wait_ge(e_ok, 3 * B - 2)
            before(pe, B, l3)
            after(pe, B, l2)
            pe.wait_ge(e_y, 2 * B + 2)
            batches(pe, B, l3)
            after(pe, B, l3)

        @block.scalar
        def _(act):
            act.preload_act_table_set("natural_log_exp_and_others")
            for_batches(act, B, att_act(act, 0, A0))

            def ln_exp(src, tmp, bias, l, l_value, done):
                nc.scalar.activation(tmp[:, 0], src, ACT.Ln, bias=bias).then_inc(l, 1)
                act.wait_ge(l, l_value)
                nc.scalar.activation(tmp[:, 1], tmp[:, 0], ACT.Exp, scale=-0.5).then_inc(done, 1)

            zbanks = (psT[0], psT[1], psO, psB)
            act.sem_inc(z_ok, 4)
            act.sem_inc(z2_ok, 2)

            def l1a(k):
                b, p = k.b, k.p
                if k.nxt and k.index not in (-1, 0):
                    act.wait_ge(ag_ps, b * 2)
                    scaled_hi(act, b + 1, 1 - p)
                if k.prev:
                    for i in range(4):
                        h, q = i // 2, i % 2
                        act.wait_ge(z_ps, b * 4 - 3 + i)
                        alone(act)
                        nc.scalar.activation(zrow(h, b - 1, q * HN, HN), zbanks[i][:], ACT.Identity,
                                             bias=b1c[:, h:h + 1]).then_inc(z_ok, 1)

            for_batches(act, B, l1a)
            act.wait_ge(bn1_mv, 1)
            ln_exp(bnmv[:, :, 1], newt[:, 0, :, 0:HB], epsc[:], bn1_l, 1, bn1_ln)
            act.wait_ge(bn1_ok, 2)

            def l1b(k):
                b, p = k.b, k.p
                if k.nxt:
                    for i in range(2 * HB):
                        z = zrow(i % HB, b + 1, i // HB * HN, HN)
                        nc.scalar.activation(z, z, ACT.Relu, bias=bnsc[:, 1, i % HB:i % HB + 1],
                                             scale=bnsc[:, 0, i % HB:i % HB + 1]).then_inc(relu_ok, 1)
                if k.cur:
                    for q in range(2):
                        act.wait_ge(z2_ps, b * 2 + 1 + q)
                        alone(act)
                        nc.scalar.activation(zrow(0, b, q * HN, HN), psS[p][:, q * HN:(q + 1) * HN], ACT.Identity,
                                             bias=b2c).then_inc(z2_ok, 1)

            for_batches(act, B, l1b)
            act.wait_ge(bn2_mv, 1)
            ln_exp(bnmv[:, 0:1, 1], newt[:, 0, :, 0:1], epsc[:], bn2_l, 1, bn2_ln)

            def norm(b, src, i, done):
                for t in range(NT):
                    n = nc.scalar.activation(xrow(b, t), src[:, t, :], ACT.Identity, bias=nbias[:, i, t:t + 1],
                                             scale=rstd[:, i, t:t + 1])
                n.then_inc(done, 1)

            def l2(k):
                b, p = k.b, k.p
                if k.nxt:
                    act.wait_ge(c_mv, b + 2)
                    ln_exp(mv[:, 0, :, 1], newt[:, 0], epsc[:], c_l, b + 2, c_ln)
                    act.wait_ge(c_nw, b + 2)
                    alone(act)
                    norm(b + 1, Yc, 0, c_x)
                    act.wait_ge(c_x, b + 2)
                    if k.cur:
                        act.wait_ge(e_ps, b * 3) if k.prev else None
                    alone(act)
                    nc.scalar.copy(FR[:, 1 - p, 0, :], xall(b + 1)).then_inc(e_hi, 1)
                if k.cur:
                    act.wait_ge(e_ps, b * 3 + 1)
                    nc.scalar.copy(UDL[:, p, 0, :], psS[0][:]).then_inc(e_ok, 1)
                if k.prev:
                    act.wait_ge(e_mv, b)
                    ln_exp(mv[:, 1, :, 1], newt[:, 1], epsc[:], e_l, b, e_ln)
                if k.cur:
                    act.wait_ge(e_ps, b * 3 + 2)
                    nc.scalar.copy(UDL[:, p, 1, :], psS[1][:]).then_inc(e_ok, 1)
                    act.wait_ge(e_ps, b * 3 + 3)
                    for q in range(2):
                        n = nc.scalar.copy(UDL[:, p, 2, q * HN:(q + 1) * HN], psT[q][:])
                    n.then_inc(e_ok, 1)
                if k.prev:
                    act.wait_ge(e_nw, b)
                    alone(act)
                    norm(b - 1, xb2[:, 1 - p], 1, e_x)

            l3 = att_act(act, 3, A3)
            before(act, B, l2)
            batches(act, B, l2)
            before(act, B, l3)
            after(act, B, l2)
            batches(act, B, l3)
            after(act, B, l3)

        @block.vector
        def _(dve):
            for_batches(dve, B, att_dve(dve, 0, A0))
            dve.sem_inc(ag_ok, 2)
            dve.sem_inc(e_y, 2)

            def l1a(k):
                b, p = k.b, k.p
                if k.prev:
                    for q in range(2):
                        cs = slice(q * HN, (q + 1) * HN)
                        dve.wait_ge(ag_ps, b * 2 - 1 + q)
                        nc.vector.tensor_tensor(agS[:, 1 - p, cs], psS[1 - p][:, cs], dinvb[:, cs],
                                                ALU.mult).then_inc(ag_ok, 1)
                if k.nxt and k.index not in (-1, 0):
                    scaled_lo(dve, b + 1, 1 - p)
                if k.prev:
                    for i in range(4):
                        h, q = i // 2, i % 2
                        dve.wait_ge(z_ok, b * 4 + 1 + i)
                        nc.vector.bn_stats(bnst2[:, bass.ds((b - 1) * 12 + h * 12 * B + q * 6, 6)],
                                           zrow(h, b - 1, q * HN, HN)).then_inc(zst_ok, 1)

            for_batches(dve, B, l1a)

            def bn_affine(n, gamma, beta, mv_done, ln_done, step, nw, ok, i):
                for h in range(n):
                    m = nc.vector.bn_aggr(bnmv[:, h, :], bnst[:, h].rearrange("p a b -> p (a b)"))
                m.then_inc(mv_done, 1)
                dve.wait_ge(mv_done, 1)
                dve.wait_ge(ln_done, 1)
                refine(dve, bnmv[:, 0:n, 1], bnmv[:, 0:n, 0], newt[:, 0, :, 0:n], bnsc[:, 4, 0:n], bnsc[:, 5, 0:n],
                       step, 0, nw, EPS)
                dve.wait_ge(nw, 1)
                nc.vector.tensor_tensor(bnsc[:, i, 0:n], bnsc[:, 4, 0:n], gamma, ALU.mult).then_inc(ok, 1)
                nc.vector.tensor_tensor(bnsc[:, i + 1, 0:n], bnsc[:, 5, 0:n], gamma, ALU.mult).then_inc(nw, 1)
                dve.wait_ge(nw, 2)
                nc.vector.tensor_tensor(bnsc[:, i + 1, 0:n], bnsc[:, i + 1, 0:n], beta, ALU.add).then_inc(ok, 1)

            dve.wait_ge(zst_ok, 4 * B)
            bn_affine(HB, g1c, be1c, bn1_mv, bn1_ln, bn1_step, bn1_nw, bn1_ok, 0)

            def l1b(k):
                if not k.cur:
                    return
                g_row = G2[:, bass.ds(k.b * N, N)]
                nc.vector.tensor_scalar(g_row, g_row, 0.0, BIG, EQ, ALU.mult).then_inc(g3_ok, 1)
                for q in range(2):
                    dve.wait_ge(z2_ok, k.b * 2 + 3 + q)
                    nc.vector.bn_stats(bnst2[:, bass.ds(k.b * 12 + q * 6, 6)],
                                       zrow(0, k.b, q * HN, HN)).then_inc(z2st_ok, 1)

            dve.wait_ge(wa_ps, 1)
            for col, src, scale in ((0, 0, -1.0), (1, 0, -0.2), (2, 1, -1.0), (3, 1, -0.2)):
                nc.vector.tensor_scalar(wa[:, col:col + 1], psO[:, src:src + 1], scale, None,
                                        ALU.mult).then_inc(wa_ok, 1)
            for_batches(dve, B, l1b)
            dve.wait_ge(z2st_ok, 2 * B)
            bn_affine(1, g2c, be2c, bn2_mv, bn2_ln, bn2_step, bn2_nw, bn2_ok, 2)
            dve.wait_ge(bn2_ok, 2)

            def l2(k):
                b, p = k.b, k.p

                def layer_stats(src, i, turn, y_sem, y_value, bn, mv_done):
                    for t in range(NT):
                        dve.wait_ge(y_sem, y_value + t // HT)
                        nc.vector.bn_stats(stats[:, i, t, :], src[:, t, :]).then_inc(bn, 1)
                    dve.wait_ge(bn, turn * NT + NT)
                    alone(dve)
                    for t in range(NT):
                        m = nc.vector.bn_aggr(mv[:, i, t, :], stats[:, i, t, :])
                    m.then_inc(mv_done, 1)

                if k.nxt:
                    if k.cur:
                        dve.wait_ge(c_ps, b + 1)
                    nc.vector.tensor_scalar(zn[:], zrow(0, b + 1, 0, N), bnsc[:, 2, 0:1], bnsc[:, 3, 0:1], ALU.mult,
                                            ALU.add).then_inc(zn_ok, 1)
                    dve.wait_ge(c_ps, b + 2)
                    if k.cur:
                        dve.wait_ge(c_x, b + 1)
                    for h in range(2):
                        nc.vector.tensor_tensor(Yc[:, h * HT:(h + 1) * HT, :].rearrange("p t c -> p (t c)"),
                                                (psO, psB)[h][:], X2[:, bass.ds((b + 1) * N + h * HN, HN)],
                                                ALU.add).then_inc(c_y, 1)
                    layer_stats(Yc, 0, b + 1, c_y, b * 2 + 3, c_bn, c_mv)
                    dve.wait_ge(c_ln, b + 2)
                    refine(dve, mv[:, 0, :, 1], mv[:, 0, :, 0], newt[:, 0], rstd[:, 0, :], nbias[:, 0, :], c_step,
                           b + 1, c_nw, EPS)
                if k.prev:
                    dve.wait_ge(e_out, b)
                    dve.wait_ge(e_xb, b)
                    y2 = xb2[:, 1 - p]
                    for h in range(2):
                        ys = y2[:, h * HT:(h + 1) * HT, :].rearrange("p t c -> p (t c)")
                        nc.vector.tensor_tensor(ys, out_banks(k)[h][:], ys, ALU.add).then_inc(e_y, 1)
                    layer_stats(y2, 1, b - 1, e_y, b * 2 + 1, e_bn, e_mv)
                if k.nxt:
                    dve.wait_ge(e_hi, b + 2)
                    nc.vector.tensor_tensor(FR[:, 1 - p, 1, :], xall(b + 1), FR[:, 1 - p, 0, :].bitcast(F32),
                                            ALU.subtract).then_inc(e_lo, 1)
                if k.prev:
                    dve.wait_ge(e_ln, b)
                    refine(dve, mv[:, 1, :, 1], mv[:, 1, :, 0], newt[:, 1], rstd[:, 1, :], nbias[:, 1, :], e_step,
                           b - 1, e_nw, EPS)

            for_batches(dve, B, l2)
            dve.wait_ge(g3_ok, NT)
            for h in range(2):
                dve.sem_inc(A3["out_ok"][h], 16)
            for_batches(dve, B, att_dve(dve, 3, A3))


def kernel(x, adj, L0_gnn_W, L0_gnn_b_lin, L0_gnn_b, L1_gnn_W1, L1_gnn_b1, L1_gnn_g1, L1_gnn_be1, L1_gnn_W2,
           L1_gnn_b2, L1_gnn_g2, L1_gnn_be2, L2_gnn_W, L2_gnn_bias, L3_gnn_W, L3_gnn_a):
    import numpy as np
    import concourse.bacc as bacc
    from concourse.bass_utils import run_bass_kernel_spmd

    def lay(v):
        return np.ascontiguousarray(np.asarray(v))

    cols = np.concatenate([np.asarray(v).reshape(-1, P) for v in (
        L0_gnn_b_lin, L1_gnn_b1, L1_gnn_g1, L1_gnn_be1, L1_gnn_b2, L1_gnn_g2, L1_gnn_be2)])
    arrays = {
        "x": lay(x), "adj": lay(adj), "adjt": lay(np.asarray(adj).T), "w0": lay(L0_gnn_W), "cols": lay(cols.T),
        "b": lay(np.asarray(L0_gnn_b)[None]), "b_lin": lay(np.asarray(L0_gnn_b_lin)[None]),
        "w1t": lay(np.asarray(L1_gnn_W1).T), "w2t": lay(np.asarray(L1_gnn_W2).T), "wl2": lay(L2_gnn_W),
        "bias2": lay(np.asarray(L2_gnn_bias)[None]), "w3": lay(L3_gnn_W), "w3t": lay(np.asarray(L3_gnn_W).T),
        "acol": lay(np.asarray(L3_gnn_a).reshape(2, P).T),
    }
    nc = bacc.Bacc("TRN2", target_bir_lowering=False, num_devices=1)
    aps = {n: nc.dram_tensor(f"{n}_dram", v.shape, mybir.dt.from_np(v.dtype), kind="ExternalInput").ap()
           for n, v in arrays.items()}
    out = nc.dram_tensor("out_dram", x.shape, F32, kind="ExternalOutput").ap()
    graph_layers(nc, aps, out)
    r = run_bass_kernel_spmd(nc, [{f"{n}_dram": v for n, v in arrays.items()}], core_ids=[0])
    return r.results[0]["out_dram"]
```

```python
from contextlib import ExitStack

import concourse.bass as bass
from concourse import mybir

P = 128
EPS = 1e-5
NEG = 1e16
BIG = 1e30
NCONST = 8
CLAMP = 1e20
F32, F32R, BF16 = mybir.dt.float32, mybir.dt.float32r, mybir.dt.bfloat16
ALU, ACT = mybir.AluOpType, mybir.ActivationFunctionType
EQ = ALU.is_equal


class Batch:

    def __init__(self, b, n, p, count):
        self.b, self.n, self.p = b, n, p
        known = isinstance(b, int)
        self.prev = not known or b >= 1
        self.cur = not known or 0 <= b < count
        self.nxt = not known or b < count - 1
        self.index = b if known else None


def before(eng, count, body):
    body(Batch(-1, -1, 1, count))


def batches(eng, count, body):
    body(Batch(0, 0, 0, count))
    with eng.Fori(0, (count - 2) // 2) as i:
        body(Batch(i * 2 + 1, i, 1, count))
        body(Batch(i * 2 + 2, i + 1, 0, count))
    body(Batch(count - 1, (count - 1) // 2, 1, count))


def after(eng, count, body):
    body(Batch(count, count // 2, 0, count))


def for_batches(eng, count, body):
    before(eng, count, body)
    batches(eng, count, body)
    after(eng, count, body)


def graph_layers(nc, a, out):
    B, N, C = a["x"].shape
    NT = N // P
    HT = NT // 2
    HN = N // 2
    HB = a["w1t"].shape[1] // P
    assert C == P and NT == 8 and HB == 2 and B == NT

    with ExitStack() as ctx:
        def sb(name, shape, dt=F32):
            return ctx.enter_context(nc.sbuf_tensor(name, shape, dt))

        def sem(name):
            return ctx.enter_context(nc.semaphore(name))

        X = sb("X", [P, B, NT, C])
        AT = sb("AT", [P, NT, N], F32R)
        agHL = sb("agHL", [P, 2, N], F32R)
        G = sb("G", [P, NT, N], BF16)
        FR = sb("FR", [P, 2, 2, N], F32R)
        arena = sb("arena", [P, 84 * 256])
        dinvb = sb("dinvb", [P, N])
        ident = sb("ident", [P, P])
        w0, w3 = sb("w0", [P, C]), sb("w3", [P, C])
        w1HL = sb("w1HL", [P, 2, HB * P], F32R)
        w1t, w2t, wl2 = sb("w1tS", [P, HB * P]), sb("w2tS", [P, HB, C]), sb("wl2S", [P, 3, C])
        w3t = sb("w3tS", [P, C])
        bias0, bias2 = sb("bias0", [P, C]), sb("bias2", [P, C])
        cols = sb("cols", [P, 12])
        acol = sb("acol", [P, 2])
        wa = sb("wa", [P, 4])
        epsc = sb("epsc", [P, 1])
        negmax = sb("negmax", [P, 2 * NT])
        sums = sb("sums", [P, 2 * NT])
        rsum = sb("rsum", [P, NT])
        small = sb("small", [P, 2, NT])
        stats = sb("stats", [P, 2, NT, 6])
        mv = sb("mv", [P, 2, NT, 2])
        newt = sb("newt", [P, 2, 4, NT])
        rstd = sb("rstd", [P, 2, NT])
        nbias = sb("nbias", [P, 2, NT])
        deg = sb("deg", [P, 4, NT])
        dinv, dtmp = sb("dinv", [P, NT]), sb("dtmp", [P, 4, NT])
        bnst = sb("bnst", [P, HB, 2 * B, 6])
        bnmv = sb("bnmv", [P, HB, 2])
        bnsc = sb("bnsc", [P, 6, HB])
        scol = sb("scol", [P, 2, NT, 4])

        def region(kb, size_kb):
            return arena[:, kb * 256:(kb + size_kb) * 256]

        bnst2 = bnst[:].rearrange("p h a b -> p (h a b)")
        xin = a["x"].rearrange("b (t p) c -> p (b t) c", p=P)
        outv = out.rearrange("b (t p) c -> p (b t) c", p=P)
        G2 = G[:].rearrange("p t n -> p (t n)")
        X2 = X[:].rearrange("p b t c -> p (b t c)")
        xs = region(0, 8).rearrange("p (q t c) -> p q t c", q=2, c=C)
        xT = region(8, 4)
        hN = region(12, 8).rearrange("p (q t c) -> p q t c", q=2, c=C)
        T = region(20, 16).rearrange("p (q n) -> p q n", q=4)
        U = region(36, 8).rearrange("p (q n) -> p q n", q=2)
        PT = region(44, 32).rearrange("p (q m n) -> p q m n", q=2, m=NT)
        OT = region(76, 4).rearrange("p (q n) -> p q n", q=2)
        Y = region(80, 4).rearrange("p (q t c) -> p q t c", q=2, c=C)
        Z1f = region(0, 64)
        DU, DD = (agHL[:, i].rearrange("p (t n) -> p t n", t=NT) for i in range(2))
        agS = region(72, 8).rearrange("p (q n) -> p q n", q=2)
        UDL = region(32, 24).rearrange("p (q k n) -> p q k n", q=2, k=3)
        zn = region(56, 4)
        diag_tmp = dinvb[:].rearrange("p (t c) -> p t c", c=C)
        Yc = region(60, 4).rearrange("p (t c) -> p t c", c=C)
        xb2 = region(64, 8).rearrange("p (q t c) -> p q t c", q=2, c=C)

        blin, b1c, g1c, be1c, b2c, g2c, be2c = (
            cols[:, 0:1], cols[:, 1:3], cols[:, 3:5], cols[:, 5:7], cols[:, 7:8], cols[:, 8:9], cols[:, 9:10])

        def ps(name, shape):
            return ctx.enter_context(nc.psum_tensor(name, shape, F32))

        psS = [ps("psS0", [P, N]), ps("psS1", [P, N])]
        psT = [ps("psT0", [P, HN]), ps("psT1", [P, HN])]
        psO, psB = ps("psO", [P, HN]), ps("psB", [P, HN])

        consts_in, ident_ok, setup_ok, g_cast, at_cast, tri_ok, h32_ok, wa_ps, wa_ok, g3_ok = (
            sem(n) for n in ("consts_in", "ident_ok", "setup_ok", "g_cast", "at_cast", "tri_ok", "h32_ok",
                             "wa_ps", "wa_ok", "g3_ok"))
        g_in = [sem(f"g_in{i}") for i in range(4)]
        at_in = [sem(f"at_in{i}") for i in range(4)]
        gate, w0_in, w1_ok, dblk_ok, lower_ok, aghi_ok, aglo_ok = (
            sem(n) for n in ("gate", "w0_in", "w1_ok", "dblk_ok", "lower_ok", "aghi_ok", "aglo_ok"))
        diag_ok, dg_ok, dg_l, dg_ln, dg_step, dinv_ok, db_ps, dinvb_ok = (
            sem(n) for n in ("diag_ok", "dg_ok", "dg_l", "dg_ln", "dg_step", "dinv_ok", "db_ps", "dinvb_ok"))
        (ahi_ok, alo_ok, ag_ps, ag_ok, z_ps, z_ok, zst_ok, bn1_mv, bn1_l, bn1_ln, bn1_step, bn1_nw, bn1_ok,
         relu_ok, z2_ps, z2_ok, z2st_ok, bn2_mv, bn2_l, bn2_ln, bn2_step, bn2_nw, bn2_ok) = (
            sem(n) for n in ("ahi_ok alo_ok ag_ps ag_ok z_ps z_ok zst_ok bn1_mv bn1_l bn1_ln bn1_step bn1_nw "
                             "bn1_ok relu_ok z2_ps z2_ok z2st_ok bn2_mv bn2_l bn2_ln bn2_step bn2_nw bn2_ok").split())
        (zn_ok, c_ps, c_y, c_bn, c_mv, c_l, c_ln, c_step, c_nw, c_x, e_hi, e_lo, e_xb, e_ps, e_ok, e_out, e_y,
         e_bn, e_mv, e_l, e_ln, e_step, e_nw, e_x) = (
            sem(n) for n in ("zn_ok c_ps c_y c_bn c_mv c_l c_ln c_step c_nw c_x e_hi e_lo e_xb e_ps e_ok e_out e_y "
                             "e_bn e_mv e_l e_ln e_step e_nw e_x").split())

        def att_semaphores(tag):
            names = ("scores_done mask_done zero_done w_done exp_done tr_done pt_done pv_done ot_done back_done "
                     "bn_done lnexp_done newt_done norm_done xt_ps xt_ok ht_ps hi_ok lo_ok hn_ps hn_ok xb_ok u_ok "
                     "s_ps s_ok sb_ps nm_ok rs_ok mv_ok l_ok newt_step y0_ok").split()
            sems = {n: sem(f"{tag}_{n}") for n in names}
            sems["x_in"] = [sem(f"{tag}_x_in{i}") for i in range(2)]
            sems["out_ok"] = [sem(f"{tag}_out_ok{i}") for i in range(2)]
            return sems

        A0, A3 = att_semaphores("l0"), att_semaphores("l3")

        block = ctx.enter_context(nc.Block())

        def v4(t):
            return t.rearrange("p (t c) -> p t c", c=C)

        def xrow(b, t):
            return X2[:, bass.ds(b * N + t * C, C)]

        def zrow(h, b, c0, n):
            return Z1f[:, bass.ds(b * N + (h * B * N + c0), n)]

        def xall(b):
            return X2[:, bass.ds(b * N, N)]

        def parts(k):
            return FR[:, B % 2] if k.index == B else agHL

        def alone(eng):
            eng.sem_inc(gate, 1)


        BACK_AT = {0: (1, 5), 3: (1, 4)}
        Y_AT = {0: (2, 6), 3: (3, 6)}
        LN_EXP_AT = {0: (3, 6), 3: (2, 5)}
        REFINE_AT = {0: (5, 7), 3: (5, 7)}
        NORM_AT = {0: (5, 7), 3: (5, 7)}

        def att_pe(pe, L, A):
            def scores(q, r):
                hi, lo = FR[:, q, 0], FR[:, q, 1]
                cs = slice(r * P, (r + 1) * P)
                for ch in range(2):
                    o = psS[r % 2][:, ch * HN:(ch + 1) * HN]
                    cc = slice(ch * HN, (ch + 1) * HN)
                    nc.tensor.matmul(o, hi[:, cs], hi[:, cc], start=True, stop=False)
                    nc.tensor.matmul(o, hi[:, cs], lo[:, cc], start=False, stop=False)
                    mm = nc.tensor.matmul(o, lo[:, cs], hi[:, cc], start=False, stop=True)
                mm.then_inc(A["scores_done"], 1)

            def body(k, steps=range(NT)):
                b, p = k.b, k.p
                for r in steps:
                    s = b * NT + r
                    if L == 0 and k.index == B and r == 1:
                        pe.wait_ge(dinv_ok, 1)
                        for t in range(NT):
                            tr = nc.tensor.transpose(psS[0][:, t * P:(t + 1) * P],
                                                     dinv[:, t:t + 1].broadcast_to([P, P]), ident[:])
                        tr.then_inc(db_ps, 1)
                    if L == 0 and (k.cur if r < NT - 1 else k.nxt):
                        if r == NT - 1:
                            pe.wait_ge(A["lo_ok"], b * 2 + 4)
                        if k.prev or (k.cur and r >= 1):
                            pe.wait_ge(A["mask_done"], s)
                        if r < NT - 1:
                            scores(p, r + 1)
                        else:
                            scores(1 - p, 0)
                    if k.prev and r == 0 or k.cur and r >= 1:
                        tile = (r - 1) % NT
                        pe.wait_ge(A["exp_done"], s)
                        for half in range(2):
                            if k.prev or r >= 2:
                                pe.wait_ge(A["pt_done"], s * 2 - 3 + half)
                            for m in range(HT):
                                blk = half * HT + m
                                tr = nc.tensor.transpose(psT[half][:, m * P:(m + 1) * P],
                                                         T[:, tile % 4, blk * P:(blk + 1) * P], ident[:])
                            tr.then_inc(A["tr_done"], 1)
                    if (k.prev and r <= 4) or (k.cur and r >= 5):
                        j = (r - 1) % 4
                        if j == 0:
                            half_no = b * 2 + (r - 1) // 4 - 1
                            pe.wait_ge(A["pt_done"], b * 16 + (r - 1) * 2)
                            if k.prev:
                                pe.wait_ge(A["ot_done"], half_no)
                            if r == 5:
                                pe.wait_ge(A["hn_ok"], b * 2 + 2)
                        q = p if r >= 5 else 1 - p
                        hq = (((r - 1) // 4) - 1) % 2
                        ms = (2 * j, 2 * j + 1)
                        if L == 3 and 1 <= r <= 4:
                            ms = ((0, 1, 2), (3, 4, 5), (6, 7), ())[j]
                        for m in ms:
                            mm = nc.tensor.matmul(psO[:], hN[:, q, m, :], PT[:, hq, m, :],
                                                  start=(m == 0), stop=(m == NT - 1))
                        if NT - 1 in ms:
                            mm.then_inc(A["pv_done"], 1)
                    if L == 3 and r == 4 and k.nxt:
                        pe.wait_ge(A["s_ok"], b + 2)
                        if k.prev:
                            pe.wait_ge(A["mask_done"], b * NT)
                        for t in range(NT):
                            tr = nc.tensor.transpose(psS[1 - p][:, t * P:(t + 1) * P],
                                                     scol[:, 1 - p, t, 2:3].broadcast_to([P, P]), ident[:])
                        tr.then_inc(A["sb_ps"], 1)
                    if r in BACK_AT[L] and k.prev:
                        h = BACK_AT[L].index(r)
                        half_no = b * 2 - 2 + h
                        pe.wait_ge(A["ot_done"], half_no + 1)
                        if r == 1 and k.nxt:
                            pe.wait_ge(A["xt_ok"], b * 2 + 3)
                        elif r == 1 and k.index == B - 1:
                            pe.wait_ge(A["hn_ok"], B * 2)
                        elif k.nxt:
                            pe.wait_ge(A["lo_ok"] if L == 0 else A["s_ok"], b * 2 + 4 if L == 0 else b + 2)
                        else:
                            pe.wait_ge(A["y0_ok"], half_no)
                        for t in range(HT):
                            tr = nc.tensor.transpose(psB[:, t * P:(t + 1) * P],
                                                     OT[:, h, t * P:(t + 1) * P], ident[:])
                        tr.then_inc(A["back_done"], 1)
                    if not k.nxt:
                        continue
                    if r in (0, 2):
                        if r == 0:
                            pe.wait_ge(A["x_in"][1 - p], (k.n + (1 if p else 0)) * 16 + 16)
                            if k.cur:
                                pe.wait_ge(A["hn_ok"], b * 2 + 2)
                        elif k.prev:
                            pe.wait_ge(A["y0_ok"], b * 2 - 1)
                        elif r == 2:
                            pe.wait_ge(A["xt_ok"], b * 2 + 3)
                        for t in range(HT):
                            tr = nc.tensor.transpose(psB[:, t * P:(t + 1) * P],
                                                     xs[:, 1 - p, r // 2 * HT + t, :], ident[:])
                        tr.then_inc(A["xt_ps"], 1)
                    if L == 0 and r in (3, 4):
                        if k.index == -1:
                            pe.wait_ge(w0_in, 32)
                        if r == 3:
                            pe.wait_ge(A["xt_ok"], b * 2 + 4)
                        else:
                            pe.wait_ge(A["lo_ok"], b * 2 + 3)
                        nc.tensor.matmul(psB[:], w0[:], xT[:, (r - 3) * HN:(r - 2) * HN],
                                         start=True, stop=True).then_inc(A["ht_ps"], 1)
                    if L == 3 and r == 3:
                        pe.wait_ge(A["xt_ok"], b * 2 + 4)
                        for t in range(NT):
                            mm = nc.tensor.matmul(psB[:, t * 4:t * 4 + 4], xT[:, t * P:(t + 1) * P], wa[:],
                                                  start=True, stop=True)
                        mm.then_inc(A["s_ps"], 1)
                    if r in (6, 7):
                        if L == 0:
                            pe.wait_ge(h32_ok, b * 2 + r - 3)
                        if r == 7:
                            pe.wait_ge(A["hn_ok"], b * 2 + 3)
                        elif k.prev:
                            pe.wait_ge(A["y0_ok"], b * 2)
                        else:
                            pe.wait_ge(A["lo_ok"] if L == 0 else A["s_ok"], b * 2 + 4 if L == 0 else b + 2)
                        for t in range(HT):
                            tt = (r - 6) * HT + t
                            o, xt = psB[:, t * P:(t + 1) * P], xT[:, tt * P:(tt + 1) * P]
                            if L == 0:
                                mm = nc.tensor.transpose(o, xt, ident[:])
                            else:
                                mm = nc.tensor.matmul(o, xt, w3[:], start=True, stop=True)
                        mm.then_inc(A["hn_ps"], 1)

            return body

        def att_act(act, L, A):
            def aux(b, p, r, cur):
                if r in (0, 2):
                    act.wait_ge(A["xt_ps"], b * 2 + 3 + r // 2)
                    if r == 0 and cur:
                        act.wait_ge(A["hn_ps"], b * 2 + 2)
                    nc.scalar.copy(xT[:, r // 2 * HN:(r // 2 + 1) * HN], psB[:]).then_inc(A["xt_ok"], 1)
                if L == 0 and r in (3, 4):
                    act.wait_ge(A["ht_ps"], b * 2 + r)
                    nc.scalar.activation(FR[:, 1 - p, 0, (r - 3) * HN:(r - 2) * HN], psB[:], ACT.Identity,
                                         bias=blin).then_inc(A["hi_ok"], 1)
                if L == 3 and r == 3:
                    act.wait_ge(A["s_ps"], b + 2)
                    nc.scalar.copy(scol[:, 1 - p, :, :].rearrange("p t k -> p (t k)"),
                                   psB[:, 0:NT * 4]).then_inc(A["s_ok"], 1)
                if r in (6, 7):
                    act.wait_ge(A["hn_ps"], b * 2 + r - 3)
                    nc.scalar.copy(hN[:, 1 - p, (r - 6) * HT:(r - 5) * HT, :], v4(psB[:])).then_inc(A["hn_ok"], 1)

            def ln_exp(b, r):
                h = LN_EXP_AT[L].index(r)
                half_no = b * 2 - 2 + h
                act.wait_ge(A["mv_ok"], half_no + 1)
                nc.scalar.activation(newt[:, h, 0, 0:HT], mv[:, h, 0:HT, 1], ACT.Ln,
                                     bias=epsc[:]).then_inc(A["l_ok"], 1)
                act.wait_ge(A["l_ok"], half_no + 1)
                nc.scalar.activation(newt[:, h, 1, 0:HT], newt[:, h, 0, 0:HT], ACT.Exp,
                                     scale=-0.5).then_inc(A["lnexp_done"], 1)

            def exponentials(b, p, r):
                if L == 3 and r % 2 == 0:
                    act.wait_ge(A["nm_ok"], b * HT + r // 2 + 1)
                act.wait_ge(A["w_done"], b * NT + r + 1)
                i = p * NT + r
                nc.scalar.activation(T[:, r % 4, :], T[:, r % 4, :], ACT.Exp, bias=negmax[:, i:i + 1],
                                     scale=-1.0, accum_out=sums[:, i:i + 1]).then_inc(A["exp_done"], 1)

            def body(k, steps=range(NT)):
                b, p = k.b, k.p
                for r in steps:
                    s = b * NT + r
                    if r >= 1 and k.nxt:
                        aux(b, p, r - 1, k.cur)
                    if r == 0 and k.cur and k.prev:
                        aux(b - 1, 1 - p, NT - 1, True)
                    if L == 0 and k.index == -1 and r >= 4:
                        for t in (2 * r - 8, 2 * r - 7):
                            act.wait_ge(g_in[t // 2], 16)
                            nc.scalar.activation(G[:, t, :], X[:, t].rearrange("p t c -> p (t c)"), ACT.Copy,
                                                 scale=-1.0, accum_out=deg[:, 0, t:t + 1]).then_inc(g_cast, 1)
                    if k.prev and r == 0 or k.cur and r >= 1:
                        j = (r - 1) % 4
                        hq = ((r - 1) // 4) % 2
                        if j == 0 and k.prev:
                            act.wait_ge(A["pv_done"], b * 2 + (r - 1) // 4 - 1)
                        for half in range(2):
                            act.wait_ge(A["tr_done"], s * 2 - 1 + half)
                            nc.scalar.copy(PT[:, hq, half * HT:(half + 1) * HT, j * P:(j + 1) * P],
                                           v4(psT[half][:])).then_inc(A["pt_done"], 1)
                    if k.cur:
                        exponentials(b, p, r)
                    if k.prev and r in LN_EXP_AT[L]:
                        ln_exp(b, r)
                    if k.prev and r in (0, 4 if L == 0 else 3):
                        h = 1 if r else 0
                        half_no = b * 2 - 2 + h
                        act.wait_ge(A["pv_done"], half_no + 1)
                        nc.scalar.copy(OT[:, h, :], psO[:]).then_inc(A["ot_done"], 1)
                    if L == 0 and k.prev and r in NORM_AT[L]:
                        h = NORM_AT[L].index(r)
                        half_no = b * 2 - 2 + h
                        act.wait_ge(A["newt_done"], half_no + 1)
                        alone(act)
                        for t in range(HT):
                            n = nc.scalar.activation(xrow(b - 1, h * HT + t), Y[:, h, t, :], ACT.Identity,
                                                     bias=nbias[:, h, t:t + 1], scale=rstd[:, h, t:t + 1])
                        n.then_inc(A["norm_done"], 1)
                    if L == 0 and k.index == 0:
                        act.wait_ge(at_in[r // 2], 16)
                        nc.scalar.activation(AT[:, r, :], X[:, r].rearrange("p t c -> p (t c)"), ACT.Copy,
                                             accum_out=deg[:, 1, r:r + 1]).then_inc(at_cast, 1)
                    if L == 0 and k.index == B - 1 and r == 4:
                        act.wait_ge(dg_ok, 2)
                        nc.scalar.activation(dtmp[:, 0], deg[:, 3, :], ACT.Ln).then_inc(dg_l, 1)
                        act.wait_ge(dg_l, 1)
                        nc.scalar.activation(dtmp[:, 1], dtmp[:, 0], ACT.Exp, scale=-0.5).then_inc(dg_ln, 1)
                    if k.index == -1 and r == NT - 1:
                        aux(b, p, NT - 1, False)
                    if L == 0 and k.index == B and r == 0:
                        act.wait_ge(dinv_ok, 1)
                        scaled_hi(act, 0, 0)
                    if L == 0 and k.index == B and r == 1:
                        act.wait_ge(A0["scores_done"], B * NT)
                        scaled_hi(act, 1, 1)
            return body

        def att_dve(dve, L, A):
            def body(k):
                b, p = k.b, k.p
                for r in range(NT):
                    s = b * NT + r
                    i = p * NT + r
                    if L == 0 and k.index == B - 1 and r == 2:
                        degrees(dve)
                    if L == 0 and k.index == B - 1 and r == 6:
                        dve.wait_ge(dg_ln, 1)
                        refine(dve, deg[:, 3, :], deg[:, 3, :], dtmp, dinv[:], small[:, 0, :], dg_step, 0, dinv_ok, 0.0)
                    if L == 0 and k.index == B and r == 4:
                        scaled_lo(dve, 1, 1)
                    if L == 0 and k.index == B and r == 1:
                        dve.wait_ge(db_ps, 1)
                        nc.vector.tensor_copy(dinvb[:], psS[0][:]).then_inc(dinvb_ok, 1)
                        scaled_lo(dve, 0, 0)
                    t_now = T[:, r % 4, :]
                    if k.cur and (k.prev or r >= 4):
                        dve.wait_ge(A["tr_done"], s * 2 - 6)
                    if L == 0 and k.cur:
                        if k.index == 0:
                            dve.wait_ge(g_cast, r + 1)
                        dve.wait_ge(A["scores_done"], s + 1)
                        nc.vector.tensor_tensor(t_now, psS[r % 2][:], G[:, r, :], ALU.mult).then_inc(A["mask_done"], 1)
                        dve.wait_ge(A["mask_done"], s + 1)
                        nc.vector.tensor_scalar(U[:, r % 2, :], t_now, 0.0, NEG, EQ,
                                                ALU.mult).then_inc(A["zero_done"], 1)
                        dve.wait_ge(A["zero_done"], s + 1)
                        alone(dve)
                        nc.vector.tensor_tensor_reduce(t_now, t_now, U[:, r % 2, :], 1.0, 3e38, ALU.add, ALU.min,
                                                       negmax[:, i:i + 1]).then_inc(A["w_done"], 1)
                    if L == 3 and k.cur:
                        if r == 0:
                            dve.wait_ge(A["sb_ps"], b + 1)
                        alone(dve)
                        nc.vector.tensor_tensor_reduce(t_now, psS[p][:], G[:, r, :], 1.0, 3e38, ALU.add, ALU.min,
                                                       small[:, 0, r:r + 1]).then_inc(A["mask_done"], 1)
                    if L == 3 and (k.cur and r >= 1 or k.prev and r == 0):
                        q, rl = (p, r - 1) if r else (1 - p, NT - 1)
                        dve.wait_ge(A["u_ok"], s)
                        nc.vector.scalar_tensor_tensor(T[:, rl % 4, :], T[:, rl % 4, :], scol[:, q, rl, 0:1],
                                                       U[:, rl % 2, :], ALU.add, ALU.min).then_inc(A["w_done"], 1)
                    if L == 3 and k.cur:
                        if r % 2:
                            pair, turn = slice(r - 1, r + 1), b * HT + r // 2 + 1
                            dve.wait_ge(A["mask_done"], s + 1)
                            nc.vector.scalar_tensor_tensor(small[:, 1, pair], small[:, 0, pair], CLAMP,
                                                           scol[:, p, pair, 0], ALU.min,
                                                           ALU.add).then_inc(A["zero_done"], 1)
                            dve.wait_ge(A["zero_done"], turn)
                            nc.vector.scalar_tensor_tensor(negmax[:, i - 1:i + 1], small[:, 1, pair], 0.2,
                                                           small[:, 1, pair], ALU.mult, ALU.min).then_inc(A["nm_ok"], 1)
                    if L == 0 and k.nxt and r in (4, 5):
                        cs = slice((r - 4) * HN, (r - 3) * HN)
                        dve.wait_ge(A["hi_ok"], b * 2 + r - 1)
                        nc.vector.scalar_tensor_tensor(FR[:, 1 - p, 1, cs], psB[:], blin,
                                                       FR[:, 1 - p, 0, cs].bitcast(F32), ALU.add,
                                                       ALU.subtract).then_inc(A["lo_ok"], 1)
                    if k.prev and r == 1:
                        dve.wait_ge(A["exp_done"], b * NT)
                        nc.vector.reciprocal(rsum[:], sums[:, (1 - p) * NT:(2 - p) * NT]).then_inc(A["rs_ok"], 1)
                    if k.prev and r in Y_AT[L]:
                        h = Y_AT[L].index(r)
                        half_no = b * 2 - 2 + h
                        dve.wait_ge(A["back_done"], half_no + 1)
                        if h == 0:
                            dve.wait_ge(A["rs_ok"], b)
                            if L == 0:
                                dve.wait_ge(A["xb_ok"], b)
                        if L == 3:
                            dve.wait_ge(A["out_ok"][h], b * 16)
                        alone(dve)
                        for t in range(HT):
                            y = nc.vector.scalar_tensor_tensor(Y[:, h, t, :], psB[:, t * P:(t + 1) * P],
                                                               rsum[:, h * HT + t:h * HT + t + 1],
                                                               xrow(b - 1, h * HT + t), ALU.mult, ALU.add)
                        y.then_inc(A["y0_ok"], 1)
                        dve.wait_ge(A["y0_ok"], half_no + 1)
                        for t in range(HT):
                            nc.vector.bn_stats(stats[:, h, t, :], Y[:, h, t, :]).then_inc(A["bn_done"], 1)
                        dve.wait_ge(A["bn_done"], half_no * HT + HT)
                        alone(dve)
                        for t in range(HT):
                            m = nc.vector.bn_aggr(mv[:, h, t, :], stats[:, h, t, :])
                        m.then_inc(A["mv_ok"], 1)
                    if k.prev and r in REFINE_AT[L]:
                        h = REFINE_AT[L].index(r)
                        half_no = b * 2 - 2 + h
                        dve.wait_ge(A["lnexp_done"], half_no + 1)
                        refine(dve, mv[:, h, 0:HT, 1], mv[:, h, 0:HT, 0], newt[:, h, :, 0:HT], rstd[:, h, 0:HT],
                               nbias[:, h, 0:HT], A["newt_step"], half_no, A["newt_done"])

            return body

        def degrees(dve):
            for t in range(NT):
                nc.vector.tensor_tensor_reduce(diag_tmp[:, t, :], G[:, t, t * P:(t + 1) * P], ident[:], 1.0, 0.0,
                                               ALU.mult, ALU.add, deg[:, 2, t:t + 1]).then_inc(diag_ok, 1)
            dve.wait_ge(diag_ok, NT)
            nc.vector.scalar_tensor_tensor(deg[:, 3, :], deg[:, 2, :], 1.0, deg[:, 1, :], ALU.add,
                                           ALU.add).then_inc(dg_ok, 1)
            dve.wait_ge(dg_ok, 1)
            nc.vector.tensor_tensor(deg[:, 3, :], deg[:, 3, :], deg[:, 0, :], ALU.subtract).then_inc(dg_ok, 1)

        def scaled_hi(act, b, p):
            act.wait_ge(A0["norm_done"], b * 2 + 2)
            alone(act)
            for t in range(NT):
                h = nc.scalar.activation(FR[:, p, 0, t * P:(t + 1) * P], xrow(b, t), ACT.Copy, scale=dinv[:, t:t + 1])
            h.then_inc(ahi_ok, 1)

        def scaled_lo(dve, b, p):
            dve.wait_ge(ahi_ok, b + 1)
            alone(dve)
            for t in range(NT):
                lo = nc.vector.scalar_tensor_tensor(FR[:, p, 1, t * P:(t + 1) * P], xrow(b, t), dinv[:, t:t + 1],
                                                    FR[:, p, 0, t * P:(t + 1) * P].bitcast(F32), ALU.mult,
                                                    ALU.subtract)
            lo.then_inc(alo_ok, 1)

        def refine(dve, var, mean, tmp, y_out, nb_out, step, turn, done, eps=EPS):
            y0, q, f = tmp[:, 1], tmp[:, 2], tmp[:, 3]
            nc.vector.tensor_tensor(q, y0, y0, ALU.mult).then_inc(step, 1)
            dve.wait_ge(step, turn * 4 + 1)
            nc.vector.scalar_tensor_tensor(f, var, eps, q, ALU.add, ALU.mult).then_inc(step, 1)
            dve.wait_ge(step, turn * 4 + 2)
            nc.vector.tensor_scalar(q, f, -0.5, 1.5, ALU.mult, ALU.add).then_inc(step, 1)
            dve.wait_ge(step, turn * 4 + 3)
            nc.vector.tensor_tensor(y_out, y0, q, ALU.mult).then_inc(step, 1)
            dve.wait_ge(step, turn * 4 + 4)
            nc.vector.scalar_tensor_tensor(nb_out, mean, -1.0, y_out, ALU.mult, ALU.mult).then_inc(done, 1)

        def out_banks(k):
            return psT if k.index == B else (psO, psB)

        @block.sync
        def _(sp):
            sp.dma_start(xs[:, 0], xin[:, 0:NT, :]).then_inc(A0["x_in"][0], 16)
            sp.dma_start(w0[:], a["w0"]).then_inc(w0_in, 16)
            sp.dma_start(cols[:, 0:10], a["cols"]).then_inc(w0_in, 16)
            adj_v = a["adj"].rearrange("(t p) m -> p t m", p=P)
            adjt_v = a["adjt"].rearrange("(t p) m -> p t m", p=P)
            stage = X[:].rearrange("p b t c -> p b (t c)")
            for i in range(4):
                sp.dma_start(stage[:, 2 * i:2 * i + 2, :], adj_v[:, 2 * i:2 * i + 2, :]).then_inc(g_in[i], 16)
            for dst, name in ((w3, "w3"), (w3t, "w3t"), (w1t, "w1t"), (acol, "acol")):
                sp.dma_start(dst[:], a[name]).then_inc(consts_in, 16)
            sp.dma_start(w2t[:], a["w2t"].rearrange("(h p) o -> p h o", p=P)).then_inc(consts_in, 16)
            sp.dma_start(wl2[:], a["wl2"].rearrange("k p o -> p k o")).then_inc(consts_in, 16)
            for dst, name in ((bias0, "b"), (bias2, "bias2")):
                sp.dma_start(dst[:], a[name].broadcast_to([P, C])).then_inc(consts_in, 16)
            sp.dma_start(xs[:, 1], xin[:, NT:2 * NT, :]).then_inc(A0["x_in"][1], 16)
            for i in range(4):
                sp.wait_ge(g_cast, 2 * i + 2)
                sp.dma_start(stage[:, 2 * i:2 * i + 2, :], adjt_v[:, 2 * i:2 * i + 2, :]).then_inc(at_in[i], 16)

            def l0(k):
                if k.nxt and k.index not in (-1, 0):
                    sp.wait_ge(A0["xt_ps"], k.b * 2)
                    sp.wait_ge(A0["xb_ok"], k.b)
                    sp.dma_start(xs[:, 1 - k.p], xin[:, bass.ds((k.b + 1) * NT, NT), :]).then_inc(
                        A0["x_in"][1 - k.p], 16)

            for_batches(sp, B, l0)

            def l3(k):
                if k.nxt:
                    sp.wait_ge(e_x, k.b + 2)
                    alone(sp)
                    if k.prev:
                        sp.wait_ge(A3["xt_ps"], k.b * 2)
                    alone(sp)
                    sp.dma_start(xs[:, 1 - k.p].rearrange("p t c -> p (t c)"), xall(k.b + 1)).then_inc(
                        A3["x_in"][1 - k.p], 16)
                if k.prev:
                    for h in range(2):
                        sp.wait_ge(A3["norm_done"], k.b * 2 - 1 + h)
                        alone(sp)
                        sp.dma_start(outv[:, bass.ds((k.b - 1) * NT + h * HT, HT), :], Y[:, h]).then_inc(
                            A3["out_ok"][h], 16)

            for_batches(sp, B, l3)
            for h in range(2):
                sp.wait_ge(A3["out_ok"][h], 16 * (B + 1))

        @block.gpsimd
        def _(pool):
            nc.gpsimd.memset(U[:, 0, 0:P], 1.0).then_inc(setup_ok, 1)
            nc.gpsimd.memset(epsc[:], EPS).then_inc(setup_ok, 1)
            pool.wait_ge(setup_ok, 1)
            nc.gpsimd.affine_select(out=ident[:], in_=U[:, 0, 0:P], compare_op=EQ, fill=0.0, base=0,
                                    pattern=[[-1, P]], channel_multiplier=1).then_inc(ident_ok, 1)
            pool.wait_ge(ident_ok, 1)

            def h_sum(k):
                for q in range(2):
                    pool.wait_ge(A0["lo_ok"], k.b * 2 + 3 + q)
                    cs = slice(q * HN, (q + 1) * HN)
                    nc.gpsimd.tensor_tensor(xT[:, cs], FR[:, 1 - k.p, 0, cs].bitcast(F32),
                                            FR[:, 1 - k.p, 1, cs].bitcast(F32), ALU.add).then_inc(h32_ok, 1)

            before(pool, B, h_sum)
            pool.wait_ge(consts_in, 16 * NCONST)
            nc.gpsimd.tensor_copy(w1HL[:, 0, :], w1t[:]).then_inc(w1_ok, 1)
            pool.wait_ge(w1_ok, 1)
            nc.gpsimd.tensor_tensor(w1HL[:, 1, :], w1t[:], w1HL[:, 0, :].bitcast(F32), ALU.subtract).then_inc(w1_ok, 1)

            def l0(k):
                if k.nxt:
                    h_sum(k)
                if k.index == 0:
                    for t in range(NT):
                        pool.wait_ge(at_cast, t + 1)
                        dblk = AT[:, t, t * P:(t + 1) * P]
                        nc.gpsimd.tensor_tensor(dblk, dblk.bitcast(F32), ident[:], ALU.add).then_inc(tri_ok, 1)
                    pool.wait_ge(tri_ok, NT)
                for bb, par in ([(0, 0)] if k.index == 0 else []) + ([(k.b + 1, 1 - k.p)] if k.nxt else []):
                    pool.wait_ge(A0["xt_ps"], bb * 2 + 2)
                    nc.gpsimd.tensor_tensor(v4(xall(bb)), xs[:, par], bias0[:].unsqueeze(1).broadcast_to([P, NT, C]),
                                            ALU.add).then_inc(A0["xb_ok"], 1)

            batches(pool, B, l0)

            pool.wait_ge(ag_ps, 2 * B)
            pool.wait_ge(z_ps, 4 * B)
            for t in range(NT):
                blk = AT[:, t, t * P:(t + 1) * P]
                nc.gpsimd.affine_select(out=DU[:, t, :], in_=blk.bitcast(F32), compare_op=ALU.is_gt, fill=0.0, base=0,
                                        pattern=[[-1, P]], channel_multiplier=1).then_inc(dblk_ok, 1)
                nc.gpsimd.tensor_tensor(DD[:, t, :], blk.bitcast(F32), ident[:], ALU.subtract).then_inc(dblk_ok, 1)
                pool.wait_ge(dblk_ok, 2 * t + 2)
                nc.gpsimd.affine_select(out=blk, in_=blk.bitcast(F32), compare_op=ALU.is_gt, fill=0.0, base=0,
                                        pattern=[[1, P]], channel_multiplier=-1).then_inc(lower_ok, 1)
                nc.gpsimd.affine_select(out=DD[:, t, :], in_=DD[:, t, :].bitcast(F32), compare_op=EQ, fill=0.0,
                                        base=0, pattern=[[-1, P]], channel_multiplier=1).then_inc(lower_ok, 1)

            def l2(k):
                if k.nxt:
                    pool.wait_ge(c_x, k.b + 2)
                    if k.prev:
                        pool.wait_ge(e_bn, k.b * NT)
                        pool.wait_ge(e_x, k.b)
                    nc.gpsimd.tensor_tensor(xb2[:, 1 - k.p], v4(xall(k.b + 1)),
                                            bias2[:].unsqueeze(1).broadcast_to([P, NT, C]), ALU.add).then_inc(e_xb, 1)

            for_batches(pool, B, l2)

            def l3(k):
                for r in range(NT):
                    s = k.b * NT + r
                    if k.cur:
                        pool.wait_ge(A3["mask_done"], s + 1)
                        if k.prev or r >= 2:
                            pool.wait_ge(A3["w_done"], s - 1)
                        alone(pool)
                        nc.gpsimd.tensor_scalar(U[:, r % 2, :], T[:, r % 4, :], 0.2, scol[:, k.p, r, 1:2],
                                                ALU.mult, ALU.add).then_inc(A3["u_ok"], 1)
                    if k.prev and r in NORM_AT[3]:
                        h = NORM_AT[3].index(r)
                        pool.wait_ge(A3["newt_done"], k.b * 2 - 1 + h)
                        alone(pool)
                        for t in range(HT):
                            n = nc.gpsimd.tensor_scalar(Y[:, h, t, :], Y[:, h, t, :], rstd[:, h, t:t + 1],
                                                        nbias[:, h, t:t + 1], ALU.mult, ALU.add)
                        n.then_inc(A3["norm_done"], 1)

            for_batches(pool, B, l3)

        @block.tensor
        def _(pe):
            pe.wait_ge(ident_ok, 1)
            for_batches(pe, B, att_pe(pe, 0, A0))
            pe.wait_ge(consts_in, 16 * NCONST)

            zbanks = (psT[0], psT[1], psO, psB)

            def l1a(k):
                b, p = k.b, k.p
                if k.cur:
                    pe.wait_ge(alo_ok, b + 1)
                    if k.index == 0:
                        pe.wait_ge(tri_ok, NT)
                        pe.wait_ge(w1_ok, 2)
                    if k.prev:
                        pe.wait_ge(ag_ok, b * 2)
                    for q in range(2):
                        for m in range(NT):
                            for part in range(2):
                                mm = nc.tensor.matmul(psS[p][:, q * HN:(q + 1) * HN], FR[:, p, part, m * P:(m + 1) * P],
                                                      AT[:, m, q * HN:(q + 1) * HN], start=(m == 0 and part == 0),
                                                      stop=(m == NT - 1 and part == 1))
                        mm.then_inc(ag_ps, 1)
                if k.prev:
                    for i in range(4):
                        h, q = i % 2, i // 2
                        pe.wait_ge(z_ok, b * 4 - 3 + i)
                        pe.wait_ge(aglo_ok, b * 2 - 1 + q)
                        for wp, part in ((0, 0), (0, 1), (1, 0)):
                            mm = nc.tensor.matmul(zbanks[i][:], w1HL[:, wp, h * P:(h + 1) * P],
                                                  parts(k)[:, part, q * HN:(q + 1) * HN], start=(wp == part),
                                                  stop=(wp == 1))
                        mm.then_inc(z_ps, 1)

            for_batches(pe, B, l1a)
            pe.wait_ge(z_ok, 4 * B + 3)
            nc.tensor.matmul(psO[:, 0:2], w3t[:], acol[:], start=True, stop=True).then_inc(wa_ps, 1)

            def l1b(k):
                if not k.cur:
                    return
                b, p = k.b, k.p
                if k.prev:
                    pe.wait_ge(z2_ok, b * 2)
                for q in range(2):
                    pe.wait_ge(relu_ok, b * 4 + q * 2 + 2)
                    for h in range(HB):
                        mm = nc.tensor.matmul(psS[p][:, q * HN:(q + 1) * HN], w2t[:, h, :],
                                              zrow(h, b, q * HN, HN), start=(h == 0), stop=(h == HB - 1))
                    mm.then_inc(z2_ps, 1)

            for_batches(pe, B, l1b)

            def adj_part(p, banks, diag, ranges, upper):
                for q in range(2):
                    first = True
                    for m in (range(NT - 1, -1, -1) if upper else range(NT)):
                        c0, c1 = ranges(m, q)
                        for part in range(2):
                            x_m = FR[:, p, part, m * P:(m + 1) * P]
                            if c1 > c0:
                                mm = nc.tensor.matmul(banks(c0, c1), x_m, AT[:, m, c0:c1], start=first, stop=True,
                                                      skip_group_check=True)
                                first = False
                        for part in range(2):
                            x_m = FR[:, p, part, m * P:(m + 1) * P]
                            if diag is not None and m // HT == q:
                                mm = nc.tensor.matmul(banks(m * P, (m + 1) * P), x_m, diag[:, m, :], start=first,
                                                      stop=True, skip_group_check=True)
                                first = False
                mm.then_inc(e_ps, 1)

            def psd(c0, c1):
                return psT[c0 // HN][:, c0 % HN:c0 % HN + c1 - c0]

            def l2(k):
                b, p = k.b, k.p
                if k.nxt:
                    pe.wait_ge(zn_ok, b + 2)
                    if k.prev:
                        pe.wait_ge(e_y, b * 2)
                    for t in range(NT):
                        tr = nc.tensor.transpose((psO if t < HT else psB)[:, t % HT * P:(t % HT + 1) * P],
                                                 zn[:, t * P:(t + 1) * P], ident[:])
                    tr.then_inc(c_ps, 1)
                if k.cur:
                    pe.wait_ge(e_lo, b + 1)
                    if k.index == 0:
                        pe.wait_ge(lower_ok, 2 * NT)
                    if k.prev:
                        pe.wait_ge(e_ok, b * 3 - 2)
                    adj_part(p, lambda c0, c1: psS[0][:, c0:c1], DU,
                             lambda m, q: (q * HN, min(m * P, (q + 1) * HN)), True)
                if k.prev:
                    pe.wait_ge(e_ok, b * 3)
                    if k.nxt:
                        pe.wait_ge(c_y, b * 2 + 4)
                    elif k.index == B - 1:
                        pe.wait_ge(e_y, b * 2)
                    ob = out_banks(k)
                    for t in range(NT):
                        for j, w in enumerate((1, 2, 0)):
                            mm = nc.tensor.matmul(ob[t // HT][:, t % HT * P:(t % HT + 1) * P],
                                                  UDL[:, 1 - p, j, t * P:(t + 1) * P], wl2[:, w, :],
                                                  start=(j == 0), stop=(j == 2))
                    mm.then_inc(e_out, 1)
                if k.cur:
                    if k.prev:
                        pe.wait_ge(e_ok, b * 3)
                    adj_part(p, lambda c0, c1: psS[1][:, c0:c1], None,
                             lambda m, q: (max(m * P, q * HN), (q + 1) * HN), False)
                    adj_part(p, psd, DD, lambda m, q: (0, 0), False)

            l3, first = att_pe(pe, 3, A3), Batch(-1, -1, 1, B)
            before(pe, B, l2)
            batches(pe, B, l2)
            pe.wait_ge(e_y, 2 * B)
            pe.wait_ge(e_ok, 3 * B - 2)
            l3(first, range(3))
            after(pe, B, l2)
            l3(first, range(3, NT))
            pe.wait_ge(e_y, 2 * B + 2)
            batches(pe, B, l3)
            after(pe, B, l3)

        @block.scalar
        def _(act):
            act.preload_act_table_set("natural_log_exp_and_others")
            for_batches(act, B, att_act(act, 0, A0))

            def ln_exp(src, tmp, bias, l, l_value, done):
                nc.scalar.activation(tmp[:, 0], src, ACT.Ln, bias=bias).then_inc(l, 1)
                act.wait_ge(l, l_value)
                nc.scalar.activation(tmp[:, 1], tmp[:, 0], ACT.Exp, scale=-0.5).then_inc(done, 1)

            zbanks = (psT[0], psT[1], psO, psB)
            act.sem_inc(z_ok, 4)

            def l1a(k):
                b, p = k.b, k.p
                if k.prev:
                    for q in range(2):
                        act.wait_ge(ag_ok, b * 2 + 1 + q)
                        alone(act)
                        nc.scalar.copy(parts(k)[:, 0, q * HN:(q + 1) * HN],
                                       agS[:, 1 - p, q * HN:(q + 1) * HN]).then_inc(aghi_ok, 1)
                if k.nxt and k.index not in (-1, 0):
                    act.wait_ge(ag_ps, b * 2)
                    scaled_hi(act, b + 1, 1 - p)
                for bb in {B - 1: (), B: (B - 2, B - 1)}.get(k.index, (b - 1,) if k.prev else ()):
                    for i in range(4):
                        h, q = i % 2, i // 2
                        act.wait_ge(z_ps, bb * 4 + 1 + i)
                        alone(act)
                        nc.scalar.activation(zrow(h, bb, q * HN, HN), zbanks[i][:], ACT.Identity,
                                             bias=b1c[:, h:h + 1]).then_inc(z_ok, 1)

            for_batches(act, B, l1a)
            act.wait_ge(bn1_mv, 1)
            ln_exp(bnmv[:, :, 1], newt[:, 0, :, 0:HB], epsc[:], bn1_l, 1, bn1_ln)
            act.wait_ge(bn1_ok, 2)

            def l1b(k):
                b, p = k.b, k.p
                if k.nxt:
                    for i in range(2 * HB):
                        z = zrow(i % HB, b + 1, i // HB * HN, HN)
                        nc.scalar.activation(z, z, ACT.Relu, bias=bnsc[:, 1, i % HB:i % HB + 1],
                                             scale=bnsc[:, 0, i % HB:i % HB + 1]).then_inc(relu_ok, 1)

            for_batches(act, B, l1b)
            act.wait_ge(bn2_mv, 1)
            ln_exp(bnmv[:, 0:1, 1], newt[:, 0, :, 0:1], epsc[:], bn2_l, 1, bn2_ln)

            def norm(b, src, i, done):
                for t in range(NT):
                    n = nc.scalar.activation(xrow(b, t), src[:, t, :], ACT.Identity, bias=nbias[:, i, t:t + 1],
                                             scale=rstd[:, i, t:t + 1])
                n.then_inc(done, 1)

            def l2(k):
                b, p = k.b, k.p
                if k.nxt:
                    act.wait_ge(c_mv, b + 2)
                    ln_exp(mv[:, 0, :, 1], newt[:, 0], epsc[:], c_l, b + 2, c_ln)
                    act.wait_ge(c_x, b + 2)
                    if k.cur and k.prev:
                        act.wait_ge(e_ps, b * 3)
                    alone(act)
                    nc.scalar.copy(FR[:, 1 - p, 0, :], xall(b + 1)).then_inc(e_hi, 1)
                if k.cur:
                    act.wait_ge(e_ps, b * 3 + 1)
                    nc.scalar.copy(UDL[:, p, 0, :], psS[0][:]).then_inc(e_ok, 1)
                if k.prev:
                    act.wait_ge(e_mv, b)
                    ln_exp(mv[:, 1, :, 1], newt[:, 1], epsc[:], e_l, b, e_ln)
                if k.cur:
                    act.wait_ge(e_ps, b * 3 + 2)
                    nc.scalar.copy(UDL[:, p, 1, :], psS[1][:]).then_inc(e_ok, 1)
                    act.wait_ge(e_ps, b * 3 + 3)
                    for q in range(2):
                        n = nc.scalar.copy(UDL[:, p, 2, q * HN:(q + 1) * HN], psT[q][:])
                    n.then_inc(e_ok, 1)
                if k.prev and k.index not in (B - 1, B):
                    act.wait_ge(e_nw, b)
                    alone(act)
                    norm(b - 1, xb2[:, 1 - p], 1, e_x)

            l3, first = att_act(act, 3, A3), Batch(-1, -1, 1, B)
            before(act, B, l2)
            batches(act, B, l2)
            l3(first, range(4))
            act.wait_ge(e_nw, B - 1)
            norm(B - 2, xb2[:, (B - 2) % 2], 1, e_x)
            after(act, B, l2)
            l3(first, range(4, NT))
            batches(act, B, l3)
            after(act, B, l3)

        @block.vector
        def _(dve):
            for_batches(dve, B, att_dve(dve, 0, A0))
            dve.sem_inc(ag_ok, 2)
            dve.sem_inc(z2_ok, 2)
            dve.sem_inc(e_y, 2)

            def l1a(k):
                b, p = k.b, k.p
                if k.prev:
                    for q in range(2):
                        cs = slice(q * HN, (q + 1) * HN)
                        dve.wait_ge(ag_ps, b * 2 - 1 + q)
                        nc.vector.tensor_tensor(agS[:, 1 - p, cs], psS[1 - p][:, cs], dinvb[:, cs],
                                                ALU.mult).then_inc(ag_ok, 1)
                    for q in range(2):
                        cs = slice(q * HN, (q + 1) * HN)
                        dve.wait_ge(aghi_ok, b * 2 - 1 + q)
                        nc.vector.tensor_tensor(parts(k)[:, 1, cs], agS[:, 1 - p, cs], parts(k)[:, 0, cs].bitcast(F32),
                                                ALU.subtract).then_inc(aglo_ok, 1)
                if k.nxt and k.index not in (-1, 0):
                    scaled_lo(dve, b + 1, 1 - p)
                for bb in {B - 1: (), B: (B - 2, B - 1)}.get(k.index, (b - 1,) if k.prev else ()):
                    for i in range(4):
                        h, q = i % 2, i // 2
                        dve.wait_ge(z_ok, bb * 4 + 5 + i)
                        nc.vector.bn_stats(bnst2[:, bass.ds(bb * 12 + h * 12 * B + q * 6, 6)],
                                           zrow(h, bb, q * HN, HN)).then_inc(zst_ok, 1)

            for_batches(dve, B, l1a)

            def bn_affine(n, gamma, beta, mv_done, ln_done, step, nw, ok, i):
                for h in range(n):
                    m = nc.vector.bn_aggr(bnmv[:, h, :], bnst[:, h].rearrange("p a b -> p (a b)"))
                m.then_inc(mv_done, 1)
                dve.wait_ge(mv_done, 1)
                dve.wait_ge(ln_done, 1)
                refine(dve, bnmv[:, 0:n, 1], bnmv[:, 0:n, 0], newt[:, 0, :, 0:n], bnsc[:, 4, 0:n], bnsc[:, 5, 0:n],
                       step, 0, nw, EPS)
                dve.wait_ge(nw, 1)
                nc.vector.tensor_tensor(bnsc[:, i, 0:n], bnsc[:, 4, 0:n], gamma, ALU.mult).then_inc(ok, 1)
                nc.vector.tensor_tensor(bnsc[:, i + 1, 0:n], bnsc[:, 5, 0:n], gamma, ALU.mult).then_inc(nw, 1)
                dve.wait_ge(nw, 2)
                nc.vector.tensor_tensor(bnsc[:, i + 1, 0:n], bnsc[:, i + 1, 0:n], beta, ALU.add).then_inc(ok, 1)

            dve.wait_ge(zst_ok, 4 * B)
            bn_affine(HB, g1c, be1c, bn1_mv, bn1_ln, bn1_step, bn1_nw, bn1_ok, 0)

            def l1b(k):
                if not k.cur:
                    return
                g_row = G2[:, bass.ds(k.b * N, N)]
                nc.vector.tensor_scalar(g_row, g_row, 0.0, BIG, EQ, ALU.mult).then_inc(g3_ok, 1)
                for q in range(2):
                    dve.wait_ge(z2_ps, k.b * 2 + 1 + q)
                    alone(dve)
                    nc.vector.tensor_scalar(zrow(0, k.b, q * HN, HN), psS[k.p][:, q * HN:(q + 1) * HN], b2c, None,
                                            ALU.add).then_inc(z2_ok, 1)
                for q in range(2):
                    dve.wait_ge(z2_ok, k.b * 2 + 3 + q)
                    nc.vector.bn_stats(bnst2[:, bass.ds(k.b * 12 + q * 6, 6)],
                                       zrow(0, k.b, q * HN, HN)).then_inc(z2st_ok, 1)

            dve.wait_ge(wa_ps, 1)
            for col, src, scale in ((0, 0, -1.0), (1, 0, -0.2), (2, 1, -1.0), (3, 1, -0.2)):
                nc.vector.tensor_scalar(wa[:, col:col + 1], psO[:, src:src + 1], scale, None,
                                        ALU.mult).then_inc(wa_ok, 1)
            for_batches(dve, B, l1b)
            dve.wait_ge(z2st_ok, 2 * B)
            bn_affine(1, g2c, be2c, bn2_mv, bn2_ln, bn2_step, bn2_nw, bn2_ok, 2)
            dve.wait_ge(bn2_ok, 2)

            def l2(k):
                b, p = k.b, k.p

                def layer_stats(src, i, turn, y_sem, y_value, bn, mv_done):
                    for t in range(NT):
                        dve.wait_ge(y_sem, y_value + t // HT)
                        nc.vector.bn_stats(stats[:, i, t, :], src[:, t, :]).then_inc(bn, 1)
                    dve.wait_ge(bn, turn * NT + NT)
                    alone(dve)
                    for t in range(NT):
                        m = nc.vector.bn_aggr(mv[:, i, t, :], stats[:, i, t, :])
                    m.then_inc(mv_done, 1)

                if k.nxt:
                    if k.cur:
                        dve.wait_ge(c_ps, b + 1)
                    nc.vector.tensor_scalar(zn[:], zrow(0, b + 1, 0, N), bnsc[:, 2, 0:1], bnsc[:, 3, 0:1], ALU.mult,
                                            ALU.add).then_inc(zn_ok, 1)
                    dve.wait_ge(c_ps, b + 2)
                    if k.cur:
                        dve.wait_ge(c_x, b + 1)
                    for h in range(2):
                        nc.vector.tensor_tensor(Yc[:, h * HT:(h + 1) * HT, :].rearrange("p t c -> p (t c)"),
                                                (psO, psB)[h][:], X2[:, bass.ds((b + 1) * N + h * HN, HN)],
                                                ALU.add).then_inc(c_y, 1)
                    layer_stats(Yc, 0, b + 1, c_y, b * 2 + 3, c_bn, c_mv)
                    dve.wait_ge(c_ln, b + 2)
                    refine(dve, mv[:, 0, :, 1], mv[:, 0, :, 0], newt[:, 0], rstd[:, 0, :], nbias[:, 0, :], c_step,
                           b + 1, c_nw, EPS)
                    dve.wait_ge(c_nw, b + 2)
                    alone(dve)
                    for t in range(NT):
                        n = nc.vector.tensor_scalar(xrow(b + 1, t), Yc[:, t, :], rstd[:, 0, t:t + 1],
                                                    nbias[:, 0, t:t + 1], ALU.mult, ALU.add)
                    n.then_inc(c_x, 1)
                if k.prev:
                    dve.wait_ge(e_out, b)
                    dve.wait_ge(e_xb, b)
                    y2 = xb2[:, 1 - p]
                    for h in range(2):
                        ys = y2[:, h * HT:(h + 1) * HT, :].rearrange("p t c -> p (t c)")
                        nc.vector.tensor_tensor(ys, out_banks(k)[h][:], ys, ALU.add).then_inc(e_y, 1)
                    layer_stats(y2, 1, b - 1, e_y, b * 2 + 1, e_bn, e_mv)
                if k.nxt:
                    dve.wait_ge(c_x, b + 2)
                    dve.wait_ge(e_hi, b + 2)
                    nc.vector.tensor_tensor(FR[:, 1 - p, 1, :], xall(b + 1), FR[:, 1 - p, 0, :].bitcast(F32),
                                            ALU.subtract).then_inc(e_lo, 1)
                if k.prev:
                    dve.wait_ge(e_ln, b)
                    refine(dve, mv[:, 1, :, 1], mv[:, 1, :, 0], newt[:, 1], rstd[:, 1, :], nbias[:, 1, :], e_step,
                           b - 1, e_nw, EPS)
                    if k.index == B:
                        dve.wait_ge(e_nw, B)
                        dve.wait_ge(e_x, B - 1)
                        for t in range(NT):
                            n = nc.vector.tensor_scalar(xrow(B - 1, t), y2[:, t, :], rstd[:, 1, t:t + 1],
                                                        nbias[:, 1, t:t + 1], ALU.mult, ALU.add)
                        n.then_inc(e_x, 1)

            for_batches(dve, B, l2)
            dve.wait_ge(g3_ok, NT)
            for h in range(2):
                dve.sem_inc(A3["out_ok"][h], 16)
            for_batches(dve, B, att_dve(dve, 3, A3))


def kernel(x, adj, L0_gnn_W, L0_gnn_b_lin, L0_gnn_b, L1_gnn_W1, L1_gnn_b1, L1_gnn_g1, L1_gnn_be1, L1_gnn_W2,
           L1_gnn_b2, L1_gnn_g2, L1_gnn_be2, L2_gnn_W, L2_gnn_bias, L3_gnn_W, L3_gnn_a):
    import numpy as np
    import concourse.bacc as bacc
    from concourse.bass_utils import run_bass_kernel_spmd

    def lay(v):
        return np.ascontiguousarray(np.asarray(v))

    cols = np.concatenate([np.asarray(v).reshape(-1, P) for v in (
        L0_gnn_b_lin, L1_gnn_b1, L1_gnn_g1, L1_gnn_be1, L1_gnn_b2, L1_gnn_g2, L1_gnn_be2)])
    arrays = {
        "x": lay(x), "adj": lay(adj), "adjt": lay(np.asarray(adj).T), "w0": lay(L0_gnn_W), "cols": lay(cols.T),
        "b": lay(np.asarray(L0_gnn_b)[None]),
        "w1t": lay(np.asarray(L1_gnn_W1).T), "w2t": lay(np.asarray(L1_gnn_W2).T), "wl2": lay(L2_gnn_W),
        "bias2": lay(np.asarray(L2_gnn_bias)[None]), "w3": lay(L3_gnn_W), "w3t": lay(np.asarray(L3_gnn_W).T),
        "acol": lay(np.asarray(L3_gnn_a).reshape(2, P).T),
    }
    nc = bacc.Bacc("TRN2", target_bir_lowering=False, num_devices=1)
    aps = {n: nc.dram_tensor(f"{n}_dram", v.shape, mybir.dt.from_np(v.dtype), kind="ExternalInput").ap()
           for n, v in arrays.items()}
    out = nc.dram_tensor("out_dram", x.shape, F32, kind="ExternalOutput").ap()
    graph_layers(nc, aps, out)
    r = run_bass_kernel_spmd(nc, [{f"{n}_dram": v for n, v in arrays.items()}], core_ids=[0])
    return r.results[0]["out_dram"]
```
